# Optimizing a Trainium2 kernel written in Bass

```python
import numpy as np
import jax
import jax.numpy as jnp

def _softmax(x, axis=-1):
    return jax.nn.softmax(x, axis=axis)

def _gelu(x):
    return jax.nn.gelu(x, approximate=True)

def _silu(x):
    return jax.nn.silu(x)

def _sigmoid(x):
    return jax.nn.sigmoid(x)

def _layernorm(x, axis=-1, eps=1e-05):
    m = jnp.mean(x, axis=axis, keepdims=True)
    v = jnp.var(x, axis=axis, keepdims=True)
    return (x - m) / jnp.sqrt(v + eps)

def _scatter_add(tgt, idx, src, axis=0):
    return tgt.at[idx].add(src)

def _segment_sum(src, seg, n):
    return jax.ops.segment_sum(src, seg, n)
kernel_name = 'mk_macaron_d1_jaxref_r8_7b7915'

def setup_inputs(seed: int=0):
    np.random.seed(seed)
    _w = jnp.asarray

    def _L0_attn_setup():
        import jax, jax.numpy as jnp
        import numpy as np
        B, L, D, H = (2, 256, 128, 16)
        d = D // H
        key = jax.random.key(seed)
        ks = jax.random.split(key, 6)
        X = jax.random.normal(ks[0], (B, L, D), dtype=jnp.float32)
        scale = 0.02
        Wq = scale * jax.random.normal(ks[1], (D, D), dtype=jnp.float32)
        Wk = scale * jax.random.normal(ks[2], (D, D), dtype=jnp.float32)
        Wv = scale * jax.random.normal(ks[3], (D, D), dtype=jnp.float32)
        Wc = scale * jax.random.normal(ks[4], (D, D), dtype=jnp.float32)
        Ltri = scale * jax.random.normal(ks[5], (H, d, d), dtype=jnp.float32)
        return {'X': X, 'Wq': Wq, 'Wk': Wk, 'Wv': Wv, 'Wc': Wc, 'Ltri': Ltri}
    _L0_attn_in = _L0_attn_setup()

    def _L0_ffn_setup():
        import jax, jax.numpy as jnp
        import numpy as np
        HIDDEN = 128
        MOE_FF = 64
        SHARED_FF = 352
        NUM_EXPERTS = 16
        TOP_K = 2
        NORM_TOPK = True
        key = jax.random.key(seed)
        ks = jax.random.split(key, 8)
        s = 0.02
        return {'layer_input': jax.random.normal(ks[0], (1, 256, HIDDEN), dtype=jnp.float32), 'gate_w': jax.random.normal(ks[1], (NUM_EXPERTS, HIDDEN), dtype=jnp.float32) * s, 'w_gate_up': jax.random.normal(ks[2], (NUM_EXPERTS, HIDDEN, 2 * MOE_FF), dtype=jnp.float32) * s, 'w_down': jax.random.normal(ks[3], (NUM_EXPERTS, MOE_FF, HIDDEN), dtype=jnp.float32) * s, 'shared_w_gate': jax.random.normal(ks[4], (SHARED_FF, HIDDEN), dtype=jnp.float32) * s, 'shared_w_up': jax.random.normal(ks[5], (SHARED_FF, HIDDEN), dtype=jnp.float32) * s, 'shared_w_down': jax.random.normal(ks[6], (HIDDEN, SHARED_FF), dtype=jnp.float32) * s, 'shared_gate_w': jax.random.normal(ks[7], (1, HIDDEN), dtype=jnp.float32) * s}
    _L0_ffn_in = _L0_ffn_setup()
    _d = {'L0_attn_X': _L0_attn_in['X'], 'L0_attn_Wq': _L0_attn_in['Wq'], 'L0_attn_Wk': _L0_attn_in['Wk'], 'L0_attn_Wv': _L0_attn_in['Wv'], 'L0_attn_Wc': _L0_attn_in['Wc'], 'L0_attn_Ltri': _L0_attn_in['Ltri'], 'L0_ffn_gate_w': _L0_ffn_in['gate_w'], 'L0_ffn_w_gate_up': _L0_ffn_in['w_gate_up'], 'L0_ffn_w_down': _L0_ffn_in['w_down'], 'L0_ffn_shared_w_gate': _L0_ffn_in['shared_w_gate'], 'L0_ffn_shared_w_up': _L0_ffn_in['shared_w_up'], 'L0_ffn_shared_w_down': _L0_ffn_in['shared_w_down'], 'L0_ffn_shared_gate_w': _L0_ffn_in['shared_gate_w']}
    _x0 = _d['L0_attn_X']
    _d['L0_attn_X'] = jax.random.normal(jax.random.fold_in(jax.random.key(seed), 1), (8, 512, 128), dtype=_x0.dtype)
    del _x0
    return _d

def reference(L0_attn_X, L0_attn_Wq, L0_attn_Wk, L0_attn_Wv, L0_attn_Wc, L0_attn_Ltri, L0_ffn_gate_w, L0_ffn_w_gate_up, L0_ffn_w_down, L0_ffn_shared_w_gate, L0_ffn_shared_w_up, L0_ffn_shared_w_down, L0_ffn_shared_gate_w):

    def _L0_attn_ref(X, Wq, Wk, Wv, Wc, Ltri):
        import jax, jax.numpy as jnp
        import numpy as np
        B, L, D, H = (2, 256, 128, 16)
        d = D // H
        Bsz, Lq, Dm = X.shape
        Q = (X @ Wq.T).reshape(Bsz, Lq, H, d)
        K = (X @ Wk.T).reshape(Bsz, Lq, H, d)
        V = (X @ Wv.T).reshape(Bsz, Lq, H, d)
        KV = jnp.einsum('blhd,blhe->blhde', K, V)
        KVc = jnp.cumsum(KV, axis=1)
        Y = jnp.einsum('blhd,blhde->blhe', Q, KVc)
        mask = jnp.tril(jnp.ones((1, d, d), dtype=X.dtype))
        Lm = Ltri * mask
        Bm = Lm @ jnp.swapaxes(Lm, -2, -1)
        Y = jnp.einsum('hed,blhd->blhe', Bm, Y)
        Y = Y.reshape(Bsz, Lq, Dm)
        return Y @ Wc.T

    def _L0_ffn_ref(layer_input, gate_w, w_gate_up, w_down, shared_w_gate, shared_w_up, shared_w_down, shared_gate_w):
        import jax, jax.numpy as jnp
        import numpy as np
        HIDDEN = 128
        MOE_FF = 64
        SHARED_FF = 352
        NUM_EXPERTS = 16
        TOP_K = 2
        NORM_TOPK = True
        B, S, D = layer_input.shape
        x = layer_input.reshape(-1, D)
        N = x.shape[0]
        shared = jax.nn.silu(x @ shared_w_gate.T) * (x @ shared_w_up.T) @ shared_w_down.T
        shared = shared * jax.nn.sigmoid(x @ shared_gate_w.T)
        logits = x @ gate_w.T
        probs = jax.nn.softmax(logits.astype(jnp.float32), axis=-1)
        rw, sel = jax.lax.top_k(probs, TOP_K)
        if NORM_TOPK:
            rw = rw / rw.sum(axis=-1, keepdims=True)
        rw = rw.astype(x.dtype)
        combine = jnp.zeros((N, NUM_EXPERTS), x.dtype).at[jnp.arange(N)[:, None], sel].set(rw)
        gu = jnp.einsum('nd,edf->nef', x, w_gate_up)
        g, h = jnp.split(gu, 2, axis=-1)
        h = jax.nn.silu(g) * h
        expert_out = jnp.einsum('nef,efd,ne->nd', h, w_down, combine)
        out = expert_out + shared
        return out.reshape(B, S, D)
    x = L0_attn_X
    x = x + 0.5 * _L0_ffn_ref(_layernorm(x, axis=-1), L0_ffn_gate_w, L0_ffn_w_gate_up, L0_ffn_w_down, L0_ffn_shared_w_gate, L0_ffn_shared_w_up, L0_ffn_shared_w_down, L0_ffn_shared_gate_w)
    x = x + _L0_attn_ref(_layernorm(x, axis=-1), L0_attn_Wq, L0_attn_Wk, L0_attn_Wv, L0_attn_Wc, L0_attn_Ltri)
    x = x + 0.5 * _L0_ffn_ref(_layernorm(x, axis=-1), L0_ffn_gate_w, L0_ffn_w_gate_up, L0_ffn_w_down, L0_ffn_shared_w_gate, L0_ffn_shared_w_up, L0_ffn_shared_w_down, L0_ffn_shared_gate_w)
    return x

_drawn_inputs = setup_inputs


def setup_inputs(seed=0):
    import zlib

    import numpy as np

    out = dict(_drawn_inputs(seed))
    spreads = {}
    factors = {'L0_attn_Wq': 8.0,
     'L0_attn_Wk': 8.0,
     'L0_attn_Wv': 8.0,
     'L0_attn_Wc': 8.0,
     'L0_attn_Ltri': 8.0,
     'L0_ffn_gate_w': 8.0,
     'L0_ffn_w_gate_up': 8.0,
     'L0_ffn_w_down': 8.0,
     'L0_ffn_shared_w_gate': 8.0,
     'L0_ffn_shared_w_up': 8.0,
     'L0_ffn_shared_w_down': 8.0,
     'L0_ffn_shared_gate_w': 8.0}
    for name, (base, spread) in spreads.items():
        noise = np.random.default_rng([zlib.crc32(name.encode()), seed]).standard_normal(out[name].shape)
        drawn = base * np.exp(spread * noise) if base else spread * noise
        out[name] = jnp.asarray(drawn.astype(out[name].dtype))
    for name, factor in factors.items():
        out[name] = (out[name] * factor).astype(out[name].dtype)
    return out
```

```python
from contextlib import ExitStack

import numpy as np

import concourse.bass as bass
from concourse import mybir
from concourse.alu_op_type import AluOpType as ALU

F32 = mybir.dt.float32
F32R = mybir.dt.float32r
U32 = mybir.dt.uint32
ACT = mybir.ActivationFunctionType

P = 128
UNITS, TOK = 8, 512
NT = TOK // P
NE, FF, SFF = 16, 64, 352
HID = NE * FF + SFF
BLOCKS = -(-HID // P)
WIDTH = [min(P, HID - P * b) for b in range(BLOCKS)]
FULL = HID // P
RW = NE + 2
HEADS, HD = 16, 8
EPS = 1e-5
LO = 64
SLOTS = 2 * BLOCKS

C_ID, C_HM, C_IO, C_SEL = 0, P, 2 * P, 2 * P + NE
C_N = C_SEL + HID

BANK_USES = ["f2.back", "at.back", "f2.turn", "f2.logits", "f2.comb",
             "f1.back", "at.turn", "at.k", "at.q", "f1.turn", "f1.logits", "f1.comb"]
FRONT1 = {"f1.turn", "f1.logits", "f1.comb"}


def bank_uses(i):
    out = list(BANK_USES)
    if i < 0:
        return [x for x in out if x in FRONT1]
    if i == 0:
        out = [x for x in out if not (x.startswith("f2.") or x == "at.back")]
    if i == 1:
        out.remove("f2.back")
    if i >= UNITS - 1:
        out = [x for x in out if x not in FRONT1]
    if i >= UNITS:
        out = [x for x in out if not (x.startswith("at.") and x != "at.back") and x != "f1.back"]
    return out


def uses_before(i, steady, name):
    k = 2 if steady else i
    n = sum(len(bank_uses(j)) for j in range(-1, k)) + (
        bank_uses(k).index(name) if k <= UNITS else 0)
    return n + (i - 2) * len(BANK_USES) if steady else n


def block_index(i, slot):
    if isinstance(i, int) and i == 0:
        return slot
    if isinstance(i, int) and i == UNITS:
        return i * SLOTS - 2 * BLOCKS + slot
    return i * SLOTS - BLOCKS + slot


def block_parity(i, slot):
    n = block_index(i, slot)
    return n % 2 if isinstance(n, int) else (slot - BLOCKS) % 2


def macaron(nc, x, wg, wu, wd, rw, wq, wk, wv, wc, lt, const, out):
    ctx = ExitStack()
    with ctx:
        def sb(name, shape, dt=F32):
            return ctx.enter_context(nc.sbuf_tensor(name, shape, dt))

        def pb(name):
            return ctx.enter_context(nc.psum_tensor(name, [P, TOK], F32))

        def sem(name):
            return ctx.enter_context(nc.semaphore(name))

        cst = sb("cst", [P, C_N])
        wg_s, wu_s = sb("wg_s", [P, HID]), sb("wu_s", [P, HID])
        wd_s = sb("wd_s", [P, BLOCKS, P])
        rw_s = sb("rw_s", [P, RW])
        wq_s, wk_s, wv_s, wc_s = (sb(n, [P, P]) for n in ("wq_s", "wk_s", "wv_s", "wc_s"))
        lt_s = sb("lt_s", [P, HD])
        wg_h, wg_l = sb("wg_h", [P, HID], F32R), sb("wg_l", [P, HID], F32R)
        wu_h, wu_l = sb("wu_h", [P, HID], F32R), sb("wu_l", [P, HID], F32R)
        rw_h, rw_l = sb("rw_h", [P, RW], F32R), sb("rw_l", [P, RW], F32R)
        wq_h, wq_l = sb("wq_h", [P, P], F32R), sb("wq_l", [P, P], F32R)
        wk_h, wk_l = sb("wk_h", [P, P], F32R), sb("wk_l", [P, P], F32R)
        wv_h, wv_l = sb("wv_h", [P, HD, P], F32R), sb("wv_l", [P, HD, P], F32R)
        sel = sb("sel", [P, HID], F32R)
        low = sb("low", [P, P])
        bmix = sb("bmix", [P, P])
        mix = sb("mix", [P, HD, P])
        mixin = sb("mixin", [P, HD, P])
        ones = sb("ones", [P, 1])
        power, eps = sb("power", [P, NT]), sb("eps", [P, NT])
        ident = cst[:, C_ID:C_ID + P]
        iota = cst[:, C_IO:C_IO + NE]

        xs = {n: sb(f"x_{n}", [P, NT, P]) for n in ("f1", "at", "f2", "out")}
        stages = ("f1", "at", "f2")
        st6 = {s: sb(f"st6_{s}", [P, NT, 6]) for s in stages}
        mv = {s: sb(f"mv_{s}", [P, NT, 2]) for s in stages}
        rstd = {s: sb(f"rstd_{s}", [P, NT]) for s in stages}
        vare = {s: sb(f"vare_{s}", [P, NT]) for s in stages}
        xn = {s: sb(f"xn_{s}", [P, NT, P]) for s in stages}
        xh = {s: sb(f"xh_{s}", [P, TOK], F32R) for s in stages}
        xl = {s: sb(f"xl_{s}", [P, TOK], F32R) for s in stages}
        yT = {s: sb(f"yT_{s}", [P, TOK]) for s in stages}
        ffns = ("f1", "f2")
        lg = {s: sb(f"lg_{s}", [P, NT, RW]) for s in ffns}
        top = {s: sb(f"top_{s}", [P, NT, 8]) for s in ffns}
        idx = {s: sb(f"idx_{s}", [P, NT, 8], U32) for s in ffns}
        idxf = {s: sb(f"idxf_{s}", [P, NT, 2]) for s in ffns}
        th = {s: sb(f"th_{s}", [P, NT, 2]) for s in ffns}
        w2 = {s: sb(f"w2_{s}", [P, NT, 2]) for s in ffns}
        eq = {s: sb(f"eq_{s}", [P, 2, NT, NE]) for s in ffns}
        cb = {s: sb(f"cb_{s}", [P, NT, NE + 1]) for s in ffns}
        ch = {s: sb(f"ch_{s}", [P, NT, P], F32R) for s in ffns}
        cT = {s: sb(f"cT_{s}", [P, TOK], F32R) for s in ffns}
        sg = sb("sg", [P, 2, TOK])
        tb = sb("tb", [P, 2, TOK])
        hb = sb("hb", [P, 2, TOK])
        kT, qT = sb("kT", [P, TOK]), sb("qT", [P, TOK])
        kv, cum, prod = (sb(n, [P, 2, TOK]) for n in ("kv", "cum", "prod"))

        pg, pc, py, pv, pa, pt = (pb(n) for n in ("pg", "pc", "py", "pv", "pa", "pt"))
        pu = [pb("pu0"), pb("pu1")]

        s_cst, s_ffw, s_atw, s_x, s_out = (sem(n) for n in ("cst_in", "ffw_in", "atw_in", "x_in", "out_done"))
        s_hi, s_lo, s_gpc = sem("w_hi"), sem("w_lo"), sem("pool_consts")
        s_low, s_bm, s_bmc, s_mixin, s_mx, s_mix = (sem(n) for n in (
            "low_done", "bm_ready", "bmix_done", "mixin_done", "mx_ready", "mix_done"))
        s_g, s_sg, s_u, s_t, s_c, s_h, s_d = (sem(n) for n in (
            "gate_ready", "silu_done", "up_ready", "t_done", "spread_ready", "h_done", "down_done"))
        s_bank = sem("bank_free")
        s_st6 = {s: sem(f"{s}_stats6") for s in stages}
        s_mv = {s: sem(f"{s}_stats") for s in stages}
        s_ve = {s: sem(f"{s}_var") for s in stages}
        s_rs = {s: sem(f"{s}_rstd") for s in stages}
        s_xn = {s: sem(f"{s}_normed") for s in stages}
        s_xt = {s: sem(f"{s}_turned") for s in stages}
        s_xh = {s: sem(f"{s}_hi") for s in stages}
        s_xl = {s: sem(f"{s}_lo") for s in stages}
        s_lgp = {s: sem(f"{s}_logits") for s in ffns}
        s_rt = {s: sem(f"{s}_route") for s in ffns}
        s_agg = sem("aggregate")
        s_hl = {s: sem(f"{s}_halves") for s in ffns}
        s_th = {s: sem(f"{s}_tanh") for s in ffns}
        s_cbp = {s: sem(f"{s}_comb_turned") for s in ffns}
        s_cT = {s: sem(f"{s}_comb_ready") for s in ffns}
        s_y = {s: sem(f"{s}_yT") for s in stages}
        s_yt = {s: sem(f"{s}_y_turned") for s in stages}
        s_res = {s: sem(f"{s}_residual") for s in stages}
        s_kp, s_k, s_qp, s_q = (sem(n) for n in ("k_ready", "k_done", "q_ready", "q_done"))
        s_v, s_kv, s_cum, s_pr, s_o = (sem(n) for n in (
            "v_ready", "kv_done", "cum_done", "prod_done", "attn_out"))
        RT = 9
        HI, LOS = 6, 6

        block = ctx.enter_context(nc.Block())

        def tiles(ap):
            return ap.rearrange("p (j c) -> p j c", c=P)

        def iterations(eng, run):
            run(-1, False)
            run(0, False)
            run(1, False)
            with eng.Fori(2, UNITS - 1) as i:
                run(i, True)
            run(UNITS - 1, False)
            run(UNITS, False)
            run(UNITS + 1, False)

        def schedule(i, steady, main, side):
            def has(unit_of):
                return steady or 0 <= i + unit_of < UNITS
            plan = {
                0: [("f2.back1", -2), ("at.a6", -1), ("at.b4", -1)],
                1: [("f2.back2", -2), ("at.a7", -1), ("at.b5", -1)],
                2: [("at.b6", -1)],
                3: [("at.b7", -1), ("at.back1", -1)],
                4: [("at.back2", -1), ("f2.stats", -1)],
                5: [("f2.norm", -1)], 6: [("f2.turn", -1)], 7: [("f2.logits", -1)],
                8: [("f2.weigh", -1)], 9: [("f2.comb", -1)],
                11: [("f1.back1", 0)],
                12: [("f1.back2", 0), ("at.stats", 0), ("f1.load", 1)],
                13: [("at.norm", 0)], 14: [("at.turn", 0)], 15: [("at.k", 0), ("at.q", 0)],
                16: [("at.a0", 0), ("f1.stats", 1)],
                17: [("at.a1", 0), ("f1.norm", 1)],
                18: [("at.a2", 0), ("at.b0", 0), ("f1.turn", 1)],
                19: [("at.a3", 0), ("at.b1", 0), ("f1.logits", 1)],
                20: [("at.a4", 0), ("at.b2", 0), ("f1.weigh", 1)],
                21: [("at.a5", 0), ("at.b3", 0), ("f1.comb", 1)],
            }
            for slot in range(SLOTS):
                late = []
                first, unit = ("f1", 0) if slot < BLOCKS else ("f2", -1)
                if has(unit):
                    late = main(first, i + unit, slot % BLOCKS, i, slot) or []
                elif slot in (0, BLOCKS):
                    main(None, None, 0, i, slot)
                for name, off in plan.get(slot, []):
                    if has(off) and name in side:
                        after = side[name](i + off, i, steady)
                        late += [after] if after else []
                for f in late:
                    f()

        def spread_v():
            return wv_s[:].rearrange("p (h e) -> p e h", e=HD).unsqueeze(3).to_broadcast([P, HD, HEADS, HD])

        def last_up(s, u):
            if isinstance(u, int) and u == 0:
                return 0
            if s == "f1":
                return BLOCKS if isinstance(u, int) and u == 1 else (u - 1) * SLOTS
            if isinstance(u, int) and u == UNITS:
                return 2 * BLOCKS * UNITS
            return u * SLOTS + BLOCKS

        @block.sync
        def _(sp):
            sp.dma_start(xs["f1"][:], x[0].rearrange("(j p) d -> p j d", p=P)).then_inc(s_x, 16)
            sp.dma_start(cst[:], const).then_inc(s_cst, 16)
            sp.dma_start(rw_s[:], rw).then_inc(s_ffw, 16)
            sp.dma_start(wg_s[:], wg).then_inc(s_ffw, 16)
            sp.dma_start(wd_s[:, 0:FULL, :], wd[0:FULL * P, :].rearrange("(b p) d -> p b d", p=P)).then_inc(s_ffw, 16)
            sp.dma_start(wd_s[0:WIDTH[-1], FULL, :], wd[FULL * P:HID, :]).then_inc(s_ffw, 16)

            def load(u, i, steady):
                sp.wait_ge(s_res["f1"], u)
                sp.dma_start(xs["f1"][:], x[u].rearrange("(j p) d -> p j d", p=P)).then_inc(s_x, 16)

            def store(u, i, steady):
                sp.wait_ge(s_res["f2"], u + 1)
                sp.dma_start(out[u].rearrange("(j p) d -> p j d", p=P), xs["out"][:]).then_inc(s_out, 16)

            def run(i, steady):
                if steady or i >= 0:
                    schedule(i, steady, lambda *a: None, {"f1.load": load, "f2.back2": store})
            iterations(sp, run)
            sp.wait_ge(s_out, 16 * UNITS)

        @block.gpsimd
        def _(pool):
            pool.memset(ones[:], 1.0).then_inc(s_gpc, 1)
            pool.memset(power[:], -0.5).then_inc(s_gpc, 1)
            pool.memset(eps[:], EPS).then_inc(s_gpc, 1)
            for s in ffns:
                pool.memset(ch[s][:].bitcast(F32), 0.0).then_inc(s_gpc, 1)
            pool.wait_ge(s_gpc, 5)

            def stats(s):
                def f(u, i, steady):
                    pool.wait_ge(s_mv[s], u + 1)
                    nc.gpsimd.tensor_tensor(vare[s][:], mv[s][:, :, 1], eps[:], ALU.add).then_inc(s_ve[s], 1)
                    pool.wait_ge(s_ve[s], u + 1)
                    nc.gpsimd.tensor_tensor(rstd[s][:], vare[s][:], power[:], ALU.pow).then_inc(s_rs[s], 1)
                return f

            def weigh(e):
                def f(u, i, steady):
                    if e == 0:
                        pool.wait_ge(s_q, u + 1)
                    pool.wait_ge(s_cum, u * HD + e + 1)
                    if steady or u > 0 or e >= 2:
                        pool.wait_ge(s_o, u * HD + e - 1)
                    nc.gpsimd.tensor_tensor(prod[:, e % 2], cum[:, e % 2], qT[:], ALU.mult).then_inc(s_pr, 1)
                return f

            side = {"f1.stats": stats("f1"), "at.stats": stats("at"), "f2.stats": stats("f2")}
            for e in range(HD):
                side[f"at.a{e}"] = weigh(e)

            def run(i, steady):
                if not steady and i == -1:
                    side["f1.stats"](0, i, steady)
                else:
                    schedule(i, steady, lambda *a: None, side)
            iterations(pool, run)

        @block.scalar
        def _(act):
            act.dma_start(wu_s[:], wu).then_inc(s_ffw, 16)
            act.dma_start(wq_s[:], wq).then_inc(s_atw, 16)
            act.dma_start(wk_s[:], wk).then_inc(s_atw, 16)
            act.dma_start(wv_s[:], wv).then_inc(s_atw, 16)
            act.dma_start(wc_s[:], wc).then_inc(s_atw, 16)
            act.dma_start(lt_s[:], lt).then_inc(s_atw, 16)

            def turn(s):
                def f(u, i, steady):
                    act.wait_ge(s_xt[s], u + 1)
                    if s == "at":
                        if steady or u > 0:
                            act.wait_ge(s_v, u * HD)
                    elif steady or u > 0:
                        act.wait_ge(s_u, last_up(s, u))
                    nc.scalar.activation(xh[s][:], pt[:], ACT.Copy).then_inc(s_xh[s], 1)
                return f

            def tanh(s):
                def f(u, i, steady):
                    act.wait_ge(s_rt[s], u * RT + 4)
                    nc.scalar.activation(th[s][:], th[s][:], ACT.Tanh, scale=0.5).then_inc(s_th[s], 1)
                return f

            def comb(s):
                def f(u, i, steady):
                    act.wait_ge(s_cbp[s], u + 1)
                    if steady or u > 0:
                        act.wait_ge(s_c, last_up(s, u))
                    nc.scalar.activation(cT[s][:], pt[:], ACT.Copy).then_inc(s_cT[s], 1)
                    act.wait_ge(s_cT[s], u + 1)
                    act.sem_inc(s_bank, 1)
                return f

            def back(s):
                def f(u, i, steady):
                    if s == "at":
                        act.wait_ge(s_o, (u + 1) * HD)
                    else:
                        act.wait_ge(s_d, last_up(s, u + 1))
                    if steady or u > 0:
                        act.wait_ge(s_yt[s], u)
                    nc.scalar.activation(yT[s][:], (pa if s == "at" else py)[:], ACT.Copy).then_inc(s_y[s], 1)
                return f

            def keys(u, i, steady):
                act.wait_ge(s_kp, u + 1)
                if steady or u > 0:
                    act.wait_ge(s_kv, u * HD)
                nc.scalar.activation(kT[:], pt[:], ACT.Copy).then_inc(s_k, 1)
                act.wait_ge(s_k, u + 1)
                act.sem_inc(s_bank, 1)

            def queries(u, i, steady):
                act.wait_ge(s_qp, u + 1)
                if steady or u > 0:
                    act.wait_ge(s_pr, u * HD)
                nc.scalar.activation(qT[:], pt[:], ACT.Copy).then_inc(s_q, 1)
                act.wait_ge(s_q, u + 1)
                act.sem_inc(s_bank, 1)

            def main(s, u, b, i, slot):
                if s is None:
                    return
                n, w = block_index(i, slot), WIDTH[b]
                act.wait_ge(s_g, n + 1)
                if not isinstance(n, int) or n >= 2:
                    act.wait_ge(s_t, n - 1)
                par = block_parity(i, slot)
                nc.scalar.activation(sg[0:w, par], pg[0:w, :], ACT.Silu).then_inc(s_sg, 1)

            side = {"at.k": keys, "at.q": queries}
            for s in stages:
                side[f"{s}.turn"], side[f"{s}.back1"] = turn(s), back(s)
            for s in ffns:
                side[f"{s}.logits"], side[f"{s}.comb"] = tanh(s), comb(s)

            def run(i, steady):
                if not steady and i == -1:
                    act.wait_ge(s_ffw, 16 * 5)
                    for dst, src in ((rw_h, rw_s), (wg_h, wg_s), (wu_h, wu_s)):
                        nc.scalar.activation(dst[:], src[:], ACT.Copy).then_inc(s_hi, 1)
                    for name in ("turn", "logits", "comb"):
                        side[f"f1.{name}"](0, i, steady)
                    act.wait_ge(s_atw, 16 * 5)
                    for dst, src in ((wq_h, wq_s), (wk_h, wk_s)):
                        nc.scalar.activation(dst[:], src[:], ACT.Copy).then_inc(s_hi, 1)
                    nc.scalar.activation(wv_h[:].rearrange("p e (h d) -> p e h d", d=HD), spread_v(),
                                         ACT.Copy).then_inc(s_hi, 1)
                else:
                    schedule(i, steady, main, side)
            iterations(act, run)

        @block.vector
        def _(dve):
            def stats(s):
                def f(u, i, steady):
                    if s == "f1":
                        dve.wait_ge(s_x, 16 * (u + 1))
                    else:
                        dve.wait_ge(s_res["at" if s == "f2" else "f1"], u + 1)
                    for j in range(NT):
                        ins = nc.vector.bn_stats(st6[s][:, j, :], xs[s][:, j, :])
                    ins.then_inc(s_st6[s], 1)
                    dve.wait_ge(s_st6[s], u + 1)
                    dve.sem_inc(s_agg, 1)
                    for j in range(NT):
                        ins = nc.vector.bn_aggr(mv[s][:, j, :], st6[s][:, j, :])
                    ins.then_inc(s_mv[s], 1)
                return f

            def norm(s):
                def f(u, i, steady):
                    dve.wait_ge(s_rs[s], u + 1)
                    if steady or u > 0:
                        dve.wait_ge(s_xt[s], u)
                    for j in range(NT):
                        ins = nc.vector.tensor_scalar(xn[s][:, j, :], xs[s][:, j, :], mv[s][:, j, 0:1],
                                                      rstd[s][:, j:j + 1], ALU.subtract, ALU.mult)
                    ins.then_inc(s_xn[s], 1)
                return f

            def turn(s):
                def f(u, i, steady):
                    dve.wait_ge(s_xh[s], u + 1)
                    nc.vector.tensor_tensor(xl[s][:], pt[:], xh[s][:].bitcast(F32), ALU.subtract).then_inc(s_xl[s], 1)
                    dve.wait_ge(s_xl[s], u + 1)
                    dve.sem_inc(s_bank, 1)
                return f

            def logits(s):
                def f(u, i, steady):
                    done = u * RT
                    dve.wait_ge(s_lgp[s], u + 1)
                    nc.vector.tensor_copy(lg[s][:], pt[:, 0:NT * RW].rearrange("p (j c) -> p j c", c=RW)).then_inc(s_rt[s], 1)
                    dve.wait_ge(s_rt[s], done + 1)
                    dve.sem_inc(s_bank, 1)
                    for j in range(NT):
                        ins = nc.vector.max(top[s][:, j, :], lg[s][:, j, 0:NE])
                    ins.then_inc(s_rt[s], 1)
                    dve.wait_ge(s_rt[s], done + 2)
                    nc.vector.tensor_tensor(th[s][:, :, 0], top[s][:, :, 0], top[s][:, :, 1], ALU.subtract).then_inc(s_rt[s], 1)
                    nc.vector.tensor_copy(th[s][:, :, 1], lg[s][:, :, NE]).then_inc(s_rt[s], 1)
                    for j in range(NT):
                        ins = nc.vector.max_index(idx[s][:, j, :], top[s][:, j, :], lg[s][:, j, 0:NE])
                    ins.then_inc(s_rt[s], 1)
                return f

            def weigh(s):
                def f(u, i, steady):
                    done = u * RT + 5
                    dve.wait_ge(s_rt[s], done)
                    nc.vector.tensor_copy(idxf[s][:], idx[s][:, :, 0:2])
                    dve.wait_ge(s_th[s], u + 1)
                    nc.vector.tensor_scalar(w2[s][:, :, 0], th[s][:, :, 0], 0.5, 0.5, ALU.mult, ALU.add)
                    nc.vector.tensor_scalar(w2[s][:, :, 1], th[s][:, :, 0], -0.5, 0.5, ALU.mult, ALU.add)
                    nc.vector.tensor_scalar(cb[s][:, :, NE], th[s][:, :, 1], 0.5, 0.5, ALU.mult,
                                            ALU.add).then_inc(s_rt[s], 1)
                    dve.wait_ge(s_rt[s], done + 1)
                    for k in range(2):
                        ins = nc.vector.tensor_tensor(
                            eq[s][:, k], iota.unsqueeze(1).to_broadcast([P, NT, NE]),
                            idxf[s][:, :, k:k + 1].to_broadcast([P, NT, NE]), ALU.is_equal)
                    ins.then_inc(s_rt[s], 1)
                    dve.wait_ge(s_rt[s], done + 2)
                    for k in range(2):
                        ins = nc.vector.tensor_tensor(
                            eq[s][:, k], eq[s][:, k], w2[s][:, :, k:k + 1].to_broadcast([P, NT, NE]), ALU.mult)
                    ins.then_inc(s_rt[s], 1)
                    dve.wait_ge(s_rt[s], done + 3)
                    nc.vector.tensor_tensor(cb[s][:, :, 0:NE], eq[s][:, 0], eq[s][:, 1], ALU.add).then_inc(s_rt[s], 1)
                    dve.wait_ge(s_rt[s], done + 4)
                    if steady or u > 0:
                        dve.wait_ge(s_cbp[s], u)
                    nc.vector.tensor_copy(ch[s][:, :, 0:NE + 1], cb[s][:]).then_inc(s_hl[s], 1)
                    dve.wait_ge(s_hl[s], 2 * u + 1)
                    nc.vector.tensor_tensor(ch[s][:, :, LO:LO + NE + 1], cb[s][:],
                                            ch[s][:, :, 0:NE + 1].bitcast(F32), ALU.subtract).then_inc(s_hl[s], 1)
                return f

            def back(s):
                after, half = {"f1": ("at", 0.5), "at": ("f2", 1.0), "f2": ("out", 0.5)}[s]

                def f(u, i, steady):
                    dve.wait_ge(s_yt[s], u + 1)
                    if steady or u > 0:
                        if s == "f2":
                            dve.wait_ge(s_out, 16 * u)
                        else:
                            dve.wait_ge(s_res[after], u)
                    nc.vector.scalar_tensor_tensor(xs[after][:], tiles(pt[:]), half, xs[s][:],
                                                   ALU.mult, ALU.add).then_inc(s_res[s], 1)
                    dve.wait_ge(s_res[s], u + 1)
                    dve.sem_inc(s_bank, 1)
                return f

            def values(e):
                def f(u, i, steady):
                    if e == 0:
                        dve.wait_ge(s_k, u + 1)
                    dve.wait_ge(s_v, u * HD + e + 1)
                    nc.vector.tensor_tensor(kv[:, e % 2], pv[:], kT[:], ALU.mult).then_inc(s_kv, 1)

                    def scan():
                        dve.wait_ge(s_kv, u * HD + e + 1)
                        if steady or u > 0 or e >= 2:
                            dve.wait_ge(s_pr, u * HD + e - 1)
                        nc.vector.tensor_tensor_scan(cum[:, e % 2], ones[:].to_broadcast([P, TOK]), kv[:, e % 2],
                                                     0.0, ALU.mult, ALU.add).then_inc(s_cum, 1)
                    return scan
                return f

            def main(s, u, b, i, slot):
                if s is None:
                    return None
                n, w, par = block_index(i, slot), WIDTH[b], block_parity(i, slot)
                dve.wait_ge(s_sg, n + 1)
                dve.wait_ge(s_u, n + 1)
                nc.vector.tensor_tensor(tb[0:w, par], pu[par][0:w, :], sg[0:w, par], ALU.mult).then_inc(s_t, 1)

                def weighted():
                    dve.wait_ge(s_t, n + 1)
                    dve.wait_ge(s_c, n + 1)
                    if not isinstance(n, int) or n >= 2:
                        dve.wait_ge(s_d, n - 1)
                    nc.vector.tensor_tensor(hb[0:w, par], pc[0:w, :], tb[0:w, par], ALU.mult).then_inc(s_h, 1)
                return [weighted]

            side = {}
            for s in stages:
                side[f"{s}.stats"], side[f"{s}.norm"], side[f"{s}.turn"] = stats(s), norm(s), turn(s)
                side[f"{s}.back2"] = back(s)
            for s in ffns:
                side[f"{s}.logits"], side[f"{s}.weigh"] = logits(s), weigh(s)
            for e in range(HD):
                side[f"at.a{e}"] = values(e)

            def low_half(dst, src, hi, n):
                dve.wait_ge(s_hi, n)
                nc.vector.tensor_tensor(dst, src, hi.bitcast(F32), ALU.subtract).then_inc(s_lo, 1)

            def run(i, steady):
                if not steady and i == -1:
                    dve.wait_ge(s_gpc, 5)
                    side["f1.stats"](0, i, steady)
                    side["f1.norm"](0, i, steady)
                    low_half(rw_l[:], rw_s[:], rw_h[:], 1)
                    side["f1.turn"](0, i, steady)
                    dve.wait_ge(s_cst, 16)
                    side["f1.logits"](0, i, steady)
                    nc.vector.tensor_copy(sel[:], cst[:, C_SEL:C_N]).then_inc(s_lo, 1)
                    side["f1.weigh"](0, i, steady)
                    low_half(wg_l[:], wg_s[:], wg_h[:], 2)
                    low_half(wu_l[:], wu_s[:], wu_h[:], 3)
                    dve.wait_ge(s_atw, 16 * 5)
                    nc.vector.tensor_tensor(low[:].rearrange("p (h e) -> p h e", e=HD),
                                            lt_s[:].unsqueeze(1).to_broadcast([P, HEADS, HD]),
                                            cst[:, C_HM:C_HM + P].rearrange("p (h e) -> p h e", e=HD),
                                            ALU.mult).then_inc(s_low, 1)
                    low_half(wq_l[:], wq_s[:], wq_h[:], 4)
                    low_half(wk_l[:], wk_s[:], wk_h[:], 5)
                    dve.wait_ge(s_hi, 6)
                    for e in range(HD):
                        ins = nc.vector.tensor_tensor(
                            wv_l[:, e, :].rearrange("p (h d) -> p h d", d=HD), spread_v()[:, e],
                            wv_h[:, e, :].bitcast(F32).rearrange("p (h d) -> p h d", d=HD), ALU.subtract)
                    ins.then_inc(s_lo, 1)
                    dve.wait_ge(s_bm, 1)
                    nc.vector.tensor_copy(bmix[:], pv[:, 0:P]).then_inc(s_bmc, 1)
                    dve.wait_ge(s_bmc, 1)
                    nc.vector.tensor_copy(
                        mixin[:].rearrange("p e (h d) -> p e h d", d=HD),
                        bmix[:].rearrange("p (h e) -> p e h", e=HD).unsqueeze(3).to_broadcast([P, HD, HEADS, HD]),
                    ).then_inc(s_mixin, 1)
                    for k, bank in enumerate((pv, pa)):
                        dve.wait_ge(s_mx, k + 1)
                        nc.vector.tensor_copy(mix[:, 4 * k:4 * k + 4, :], tiles(bank[:])).then_inc(s_mix, 1)
                else:
                    schedule(i, steady, main, side)
            iterations(dve, run)

        @block.tensor
        def _(pe):
            def three(dst, wh, wl, h, l):
                nc.tensor.matmul(dst, wh, h, start=True, stop=False)
                nc.tensor.matmul(dst, wh, l, start=False, stop=False)
                return nc.tensor.matmul(dst, wl, h, start=False, stop=True)

            def bank(i, steady, name):
                pe.wait_ge(s_bank, uses_before(i, steady, name))

            def turn(s):
                def f(u, i, steady):
                    pe.wait_ge(s_xn[s], u + 1)
                    if steady or i >= 0:
                        bank(i, steady, f"{s}.turn")
                    for j in range(NT):
                        ins = nc.tensor.transpose(pt[:, j * P:(j + 1) * P], xn[s][:, j, :], ident)
                    ins.then_inc(s_xt[s], 1)
                return f

            def logits(s):
                def f(u, i, steady):
                    pe.wait_ge(s_xl[s], u + 1)
                    bank(i, steady, f"{s}.logits")
                    for j in range(NT):
                        h, l = xh[s][:, j * P:(j + 1) * P], xl[s][:, j * P:(j + 1) * P]
                        dst = pt[:, j * RW:(j + 1) * RW]
                        nc.tensor.matmul(dst, h, rw_h[:], start=True, stop=False)
                        nc.tensor.matmul(dst, h, rw_l[:], start=False, stop=False)
                        ins = nc.tensor.matmul(dst, l, rw_h[:], start=False, stop=True)
                    ins.then_inc(s_lgp[s], 1)
                return f

            def comb(s):
                def f(u, i, steady):
                    pe.wait_ge(s_hl[s], 2 * u + 2)
                    bank(i, steady, f"{s}.comb")
                    for j in range(NT):
                        ins = nc.tensor.transpose(pt[:, j * P:(j + 1) * P], ch[s][:, j, :].bitcast(F32), ident)
                    ins.then_inc(s_cbp[s], 1)
                return f

            def back(s):
                def f(u, i, steady):
                    pe.wait_ge(s_y[s], u + 1)
                    bank(i, steady, f"{s}.back")
                    for j in range(NT):
                        ins = nc.tensor.transpose(pt[:, j * P:(j + 1) * P], yT[s][:, j * P:(j + 1) * P], ident)
                    ins.then_inc(s_yt[s], 1)
                return f

            def keys(u, i, steady):
                pe.wait_ge(s_xl["at"], u + 1)
                bank(i, steady, "at.k")
                three(pt[:], wk_h[:], wk_l[:], xh["at"][:], xl["at"][:]).then_inc(s_kp, 1)

            def queries(u, i, steady):
                bank(i, steady, "at.q")
                three(pt[:], wq_h[:], wq_l[:], xh["at"][:], xl["at"][:]).then_inc(s_qp, 1)

            def values(e):
                def f(u, i, steady):
                    if steady or u > 0 or e > 0:
                        pe.wait_ge(s_kv, u * HD + e)
                    three(pv[:], wv_h[:, e, :], wv_l[:, e, :], xh["at"][:], xl["at"][:]).then_inc(s_v, 1)
                return f

            def mixed(e):
                def f(u, i, steady):
                    pe.wait_ge(s_pr, u * HD + e + 1)
                    if e == 0 and (steady or u > 0):
                        pe.wait_ge(s_y["at"], u)
                    nc.tensor.matmul(pa[:], mix[:, e, :], prod[:, e % 2], start=e == 0,
                                     stop=e == HD - 1).then_inc(s_o, 1)
                return f

            pending = []

            def down():
                if not pending:
                    return
                s, u, b, n, par = pending.pop()
                w = WIDTH[b]
                pe.wait_ge(s_h, n + 1)
                if b == 0 and not (isinstance(n, int) and n == 0):
                    if s == "f2":
                        pe.wait_ge(s_y["f1"], u + 2 if not (isinstance(u, int) and u == UNITS - 1) else UNITS)
                    elif not (isinstance(u, int) and u == 1):
                        pe.wait_ge(s_y["f2"], u - 1)
                    else:
                        pe.wait_ge(s_y["f1"], 1)
                if b == 0 and isinstance(u, int) and s == "f2" and u == UNITS - 1:
                    pe.wait_ge(s_y["f2"], UNITS - 1)
                nc.tensor.matmul(py[:], wd_s[0:w, b, :], hb[0:w, par], start=b == 0,
                                 stop=b == BLOCKS - 1).then_inc(s_d, 1)

            def main(s, u, b, i, slot):
                if s is None:
                    down()
                    return
                n, w, par = block_index(i, slot), WIDTH[b], block_parity(i, slot)
                cols = slice(b * P, b * P + w)
                first = isinstance(n, int) and n == 0
                if b == 0:
                    pe.wait_ge(s_xl[s], u + 1)
                if not first:
                    pe.wait_ge(s_sg, n)
                three(pg[0:w, :], wg_h[:, cols], wg_l[:, cols], xh[s][:], xl[s][:]).then_inc(s_g, 1)
                if not isinstance(n, int) or n >= 2:
                    pe.wait_ge(s_t, n - 1)
                three(pu[par][0:w, :], wu_h[:, cols], wu_l[:, cols], xh[s][:], xl[s][:]).then_inc(s_u, 1)
                if b == 0:
                    pe.wait_ge(s_cT[s], u + 1)
                if not first:
                    pe.wait_ge(s_h, n)
                nc.tensor.matmul(pc[0:w, :], sel[:, cols], cT[s][:], start=True, stop=True).then_inc(s_c, 1)
                down()
                pending.append((s, u, b, n, par))

            side = {"at.k": keys, "at.q": queries}
            for s in stages:
                side[f"{s}.turn"], side[f"{s}.back2"] = turn(s), back(s)
            for s in ffns:
                side[f"{s}.logits"], side[f"{s}.comb"] = logits(s), comb(s)
            for e in range(HD):
                side[f"at.a{e}"], side[f"at.b{e}"] = values(e), mixed(e)

            def run(i, steady):
                if not steady and i == -1:
                    pe.wait_ge(s_cst, 16)
                    side["f1.turn"](0, i, steady)
                    pe.wait_ge(s_lo, 1)
                    side["f1.logits"](0, i, steady)
                    side["f1.comb"](0, i, steady)
                    pe.wait_ge(s_low, 1)
                    nc.tensor.matmul(pv[:, 0:P], low[:], low[:], start=True, stop=True).then_inc(s_bm, 1)
                    pe.wait_ge(s_mixin, 1)
                    for k, bank_ in enumerate((pv, pa)):
                        for e in range(4 * k, 4 * k + 4):
                            ins = nc.tensor.matmul(bank_[:, (e % 4) * P:(e % 4 + 1) * P], mixin[:, e, :], wc_s[:],
                                                   start=True, stop=True)
                        ins.then_inc(s_mx, 1)
                    pe.wait_ge(s_lo, 7)
                    pe.wait_ge(s_mix, 2)
                    return
                if steady or i == UNITS - 1:
                    pending[:] = [("f2", i - 2, BLOCKS - 1, block_index(i, -1), block_parity(i, -1))]
                schedule(i, steady, main, side)
            iterations(pe, run)


_ARGS = ["x", "wg", "wu", "wd", "rw", "wq", "wk", "wv", "wc", "lt", "const"]


def constants():
    c = np.zeros((P, C_N), np.float32)
    c[:, C_ID:C_ID + P] = np.eye(P)
    for h in range(HEADS):
        for k in range(HD):
            for e in range(k, HD):
                c[h * HD + k, C_HM + h * HD + e] = 1.0
    c[:, C_IO:C_IO + NE] = np.arange(NE)
    for m in range(HID):
        k = min(m // FF, NE)
        c[k, C_SEL + m] = c[LO + k, C_SEL + m] = 1.0
    return c


def kernel(L0_attn_X, L0_attn_Wq, L0_attn_Wk, L0_attn_Wv, L0_attn_Wc, L0_attn_Ltri, L0_ffn_gate_w,
           L0_ffn_w_gate_up, L0_ffn_w_down, L0_ffn_shared_w_gate, L0_ffn_shared_w_up,
           L0_ffn_shared_w_down, L0_ffn_shared_gate_w):
    import concourse.bacc as bacc
    from concourse.bass_utils import run_bass_kernel_spmd as run

    gu = np.asarray(L0_ffn_w_gate_up)
    router = np.zeros((P, RW), np.float32)
    router[:, 0:NE] = np.asarray(L0_ffn_gate_w).T
    router[:, NE:NE + 1] = np.asarray(L0_ffn_shared_gate_w).T
    data = [
        np.asarray(L0_attn_X),
        np.concatenate([gu[:, :, 0:FF].transpose(1, 0, 2).reshape(P, -1), np.asarray(L0_ffn_shared_w_gate).T], 1),
        np.concatenate([gu[:, :, FF:].transpose(1, 0, 2).reshape(P, -1), np.asarray(L0_ffn_shared_w_up).T], 1),
        np.concatenate([np.asarray(L0_ffn_w_down).reshape(-1, P), np.asarray(L0_ffn_shared_w_down).T], 0),
        router,
        np.asarray(L0_attn_Wq).T, np.asarray(L0_attn_Wk).T, np.asarray(L0_attn_Wv).T, np.asarray(L0_attn_Wc).T,
        np.asarray(L0_attn_Ltri).transpose(0, 2, 1).reshape(P, HD),
        constants(),
    ]
    nc = bacc.Bacc("TRN2", target_bir_lowering=False, num_devices=1)
    arrays, args = {}, []
    for name, a in zip(_ARGS, data):
        a = np.ascontiguousarray(a)
        arrays[f"in_{name}"] = a
        args.append(nc.dram_tensor(f"in_{name}", a.shape, mybir.dt.from_np(a.dtype), kind="ExternalInput").ap())
    args.append(nc.dram_tensor("out_0", (UNITS, TOK, P), F32, kind="ExternalOutput").ap())
    macaron(nc, *args)
    return run(nc, [arrays], core_ids=[0]).results[0]["out_0"]
```

```python
from contextlib import ExitStack

import numpy as np

import concourse.bass as bass
from concourse import mybir
from concourse.alu_op_type import AluOpType as ALU

F32 = mybir.dt.float32
F32R = mybir.dt.float32r
U32 = mybir.dt.uint32
ACT = mybir.ActivationFunctionType

P = 128
UNITS, TOK = 8, 512
NT = TOK // P
NE, FF, SFF = 16, 64, 352
HID = NE * FF + SFF
BLOCKS = -(-HID // P)
WIDTH = [min(P, HID - P * b) for b in range(BLOCKS)]
FULL = HID // P
RW = NE + 2
HEADS, HD = 16, 8
EPS = 1e-5
LO = 64
SLOTS = 2 * BLOCKS
BUFS = 4
REUSE = 3

C_ID, C_HM, C_IO, C_SEL = 0, P, 2 * P, 2 * P + NE
C_N = C_SEL + HID

BANK_USES = ["f2.back", "at.back", "f2.turn", "f2.logits", "f2.comb", "f1.turn", "f1.logits",
             "f1.back", "f1.comb", "at.turn", "at.k", "at.q"]
FRONT1 = {"f1.turn", "f1.logits", "f1.comb"}


def bank_uses(i):
    out = list(BANK_USES)
    if i < 0:
        return [x for x in out if x in FRONT1]
    if i == 0:
        out = [x for x in out if not (x.startswith("f2.") or x == "at.back")]
    if i == 1:
        out.remove("f2.back")
    if i >= UNITS - 1:
        out = [x for x in out if x not in FRONT1]
    if i >= UNITS:
        out = [x for x in out if not (x.startswith("at.") and x != "at.back") and x != "f1.back"]
    return out


def uses_before(i, steady, name):
    k = 2 if steady else i
    n = sum(len(bank_uses(j)) for j in range(-1, k)) + (
        bank_uses(k).index(name) if k <= UNITS else 0)
    return n + (i - 2) * len(BANK_USES) if steady else n


def block_index(i, slot):
    if isinstance(i, int) and i == 0:
        return slot
    if isinstance(i, int) and i == UNITS:
        return i * SLOTS - 2 * BLOCKS + slot
    return i * SLOTS - BLOCKS + slot


def block_of(i, steady, slot):
    if slot < 0:
        i, slot = i - 1, slot + SLOTS
    stage, unit = ("f1", i) if slot < BLOCKS else ("f2", i - 1)
    if not steady and not 0 <= unit < UNITS:
        return None
    b = slot % BLOCKS
    n = block_index(i, slot)
    return stage, unit, b, n, WIDTH[b], n % 2 if isinstance(n, int) else (slot - BLOCKS) % 2


def macaron(nc, x, wg, wu, wd, rw, wq, wk, wv, wc, lt, const, out):
    ctx = ExitStack()
    with ctx:
        def sb(name, shape, dt=F32):
            return ctx.enter_context(nc.sbuf_tensor(name, shape, dt))

        def pb(name):
            return ctx.enter_context(nc.psum_tensor(name, [P, TOK], F32))

        def sem(name):
            return ctx.enter_context(nc.semaphore(name))

        cst = sb("cst", [P, C_N])
        wg_s, wu_s = sb("wg_s", [P, HID]), sb("wu_s", [P, HID])
        wd_s = sb("wd_s", [P, BLOCKS, P])
        wd_h, wd_l = sb("wd_h", [P, BLOCKS, P], F32R), sb("wd_l", [P, BLOCKS, P], F32R)
        rw_s = sb("rw_s", [P, RW])
        wq_s, wk_s, wv_s, wc_s = (sb(n, [P, P]) for n in ("wq_s", "wk_s", "wv_s", "wc_s"))
        lt_s = sb("lt_s", [P, HD])
        wg_h, wg_l = sb("wg_h", [P, HID], F32R), sb("wg_l", [P, HID], F32R)
        wu_h, wu_l = sb("wu_h", [P, HID], F32R), sb("wu_l", [P, HID], F32R)
        rw_hl = sb("rw_hl", [P, 2, RW], F32R)
        wq_h, wq_l = sb("wq_h", [P, P], F32R), sb("wq_l", [P, P], F32R)
        wk_h, wk_l = sb("wk_h", [P, P], F32R), sb("wk_l", [P, P], F32R)
        wv_h, wv_l = sb("wv_h", [P, HD, P], F32R), sb("wv_l", [P, HD, P], F32R)
        sel = sb("sel", [P, HID], F32R)
        low = sb("low", [P, P])
        bmix = sb("bmix", [P, P])
        mix = sb("mix", [P, HD, P])
        mixin = sb("mixin", [P, HD, P])
        ones = sb("ones", [P, 1])
        power, eps = sb("power", [P, NT]), sb("eps", [P, NT])
        ident = cst[:, C_ID:C_ID + P]
        iota = cst[:, C_IO:C_IO + NE]

        xs = {n: sb(f"x_{n}", [P, NT, P]) for n in ("f1", "at", "f2", "out")}
        x_next = sb("x_next", [P, NT, P])
        x_read = {"f1": x_next, "at": xs["at"], "f2": xs["f2"]}
        stages = ("f1", "at", "f2")
        st6 = {s: sb(f"st6_{s}", [P, NT, 6]) for s in stages}
        mv = {s: sb(f"mv_{s}", [P, NT, 2]) for s in stages}
        rstd = {s: sb(f"rstd_{s}", [P, NT]) for s in stages}
        vare = {s: sb(f"vare_{s}", [P, NT]) for s in stages}
        xn = {s: sb(f"xn_{s}", [P, NT, P]) for s in stages}
        xh = {s: sb(f"xh_{s}", [P, TOK], F32R) for s in stages}
        xl = {s: sb(f"xl_{s}", [P, TOK], F32R) for s in stages}
        yT = {s: sb(f"yT_{s}", [P, TOK]) for s in stages}
        ffns = ("f1", "f2")
        lg = {s: sb(f"lg_{s}", [P, NT, RW]) for s in ffns}
        top = {s: sb(f"top_{s}", [P, NT, 8]) for s in ffns}
        idx = {s: sb(f"idx_{s}", [P, NT, 8], U32) for s in ffns}
        idxf = {s: sb(f"idxf_{s}", [P, NT, 2]) for s in ffns}
        th = {s: sb(f"th_{s}", [P, NT, 2]) for s in ffns}
        w2 = {s: sb(f"w2_{s}", [P, NT, 2]) for s in ffns}
        eq = {s: sb(f"eq_{s}", [P, 2, NT, NE]) for s in ffns}
        cb = {s: sb(f"cb_{s}", [P, NT, NE + 1]) for s in ffns}
        ch = {s: sb(f"ch_{s}", [P, NT, P], F32R) for s in ffns}
        cT = {s: sb(f"cT_{s}", [P, TOK], F32R) for s in ffns}
        sg, cs, sc, h32 = (sb(n, [P, BUFS, TOK]) for n in ("sg", "cs", "sc", "h32"))
        hh, hl = (sb(n, [P, BUFS, TOK], F32R) for n in ("hh", "hl"))
        kT, qT = sb("kT", [P, TOK]), sb("qT", [P, TOK])
        kv, cum, prod = (sb(n, [P, 2, TOK]) for n in ("kv", "cum", "prod"))

        pg, pc, py, pv, pa, pt = (pb(n) for n in ("pg", "pc", "py", "pv", "pa", "pt"))
        pu = [pb("pu0"), pb("pu1")]

        s_cst, s_ffw, s_atw, s_x, s_out = (sem(n) for n in ("cst_in", "ffw_in", "atw_in", "x_in", "out_done"))
        s_hi, s_lo, s_gpc = sem("w_hi"), sem("w_lo"), sem("pool_consts")
        s_low, s_bm, s_bmc, s_mixin, s_mx, s_mix = (sem(n) for n in (
            "low_done", "bm_ready", "bmix_done", "mixin_done", "mx_ready", "mix_done"))
        s_g, s_sg, s_u, s_c, s_cs, s_sc, s_h, s_hh, s_hlo, s_d = (sem(n) for n in (
            "gate_ready", "silu_done", "up_ready", "spread_ready", "spread_done", "scaled_done",
            "h_done", "h_hi", "h_lo", "down_done"))
        s_bank = sem("bank_free")
        s_st6 = {s: sem(f"{s}_stats6") for s in stages}
        s_mv = {s: sem(f"{s}_stats") for s in stages}
        s_ve = {s: sem(f"{s}_var") for s in stages}
        s_rs = {s: sem(f"{s}_rstd") for s in stages}
        s_xn = {s: sem(f"{s}_normed") for s in stages}
        s_xt = {s: sem(f"{s}_turned") for s in stages}
        s_xh = {s: sem(f"{s}_hi") for s in stages}
        s_xl = {s: sem(f"{s}_lo") for s in stages}
        s_lgp = {s: sem(f"{s}_logits") for s in ffns}
        s_rt = {s: sem(f"{s}_route") for s in ffns}
        s_keep = sem("input_kept")
        s_agg = sem("aggregate")
        s_hl = {s: sem(f"{s}_halves") for s in ffns}
        s_th = {s: sem(f"{s}_tanh") for s in ffns}
        s_cbp = {s: sem(f"{s}_comb_turned") for s in ffns}
        s_cT = {s: sem(f"{s}_comb_ready") for s in ffns}
        s_y = {s: sem(f"{s}_yT") for s in stages}
        s_yt = {s: sem(f"{s}_y_turned") for s in stages}
        s_res = {s: sem(f"{s}_residual") for s in stages}
        s_kp, s_k, s_qp, s_q = (sem(n) for n in ("k_ready", "k_done", "q_ready", "q_done"))
        s_v, s_kv, s_cum, s_pr, s_o = (sem(n) for n in (
            "v_ready", "kv_done", "cum_done", "prod_done", "attn_out"))
        RT = 9

        block = ctx.enter_context(nc.Block())

        def tiles(ap):
            return ap.rearrange("p (j c) -> p j c", c=P)

        def iterations(eng, run):
            run(-1, False)
            run(0, False)
            run(1, False)
            with eng.Fori(2, UNITS - 1) as i:
                run(i, True)
            run(UNITS - 1, False)
            run(UNITS, False)
            run(UNITS + 1, False)

        def schedule(i, steady, main, side):
            plan = {
                0: [("f1.load", 1), ("at.a5", -1), ("at.p4", -1), ("at.b3", -1)],
                1: [("at.a6", -1), ("at.p5", -1), ("at.b4", -1)],
                2: [("f2.back1", -2), ("at.a7", -1), ("at.p6", -1), ("at.b5", -1)],
                3: [("f2.back2", -2), ("at.p7", -1), ("at.b6", -1)],
                4: [("at.b7", -1), ("at.back1", -1)],
                5: [("at.back2", -1), ("f2.stats", -1)],
                6: [("f2.norm", -1)], 7: [("f2.turn", -1)], 8: [("f2.logits", -1)],
                9: [("f2.weigh", -1)],
                10: [("f2.comb", -1), ("f1.stats", 1)],
                11: [("f1.norm", 1)],
                12: [("f1.turn", 1)],
                13: [("f1.logits", 1), ("f1.back1", 0)],
                14: [("f1.back2", 0), ("at.stats", 0), ("f1.weigh", 1)],
                15: [("at.norm", 0), ("f1.comb", 1), ("f1.keep", 1)],
                16: [("at.turn", 0)],
                17: [("at.k", 0), ("at.a0", 0)],
                18: [("at.q", 0), ("at.a1", 0), ("at.p0", 0)],
                19: [("at.a2", 0), ("at.p1", 0), ("at.b0", 0)],
                20: [("at.a3", 0), ("at.p2", 0), ("at.b1", 0)],
                21: [("at.a4", 0), ("at.p3", 0), ("at.b2", 0)],
            }
            for slot in range(SLOTS):
                late = [main(i, steady, slot)]
                for name, off in plan.get(slot, []):
                    if (steady or 0 <= i + off < UNITS) and name in side:
                        late.append(side[name](i + off, i, steady))
                for f in late:
                    if f:
                        f()

        def spread_v():
            return wv_s[:].rearrange("p (h e) -> p e h", e=HD).unsqueeze(3).to_broadcast([P, HD, HEADS, HD])

        def last_up(s, u):
            if isinstance(u, int) and u == 0:
                return 0
            if s == "f1":
                return BLOCKS if isinstance(u, int) and u == 1 else (u - 1) * SLOTS
            if isinstance(u, int) and u == UNITS:
                return 2 * BLOCKS * UNITS
            return u * SLOTS + BLOCKS

        @block.sync
        def _(sp):
            sp.dma_start(x_next[:], x[0].rearrange("(j p) d -> p j d", p=P)).then_inc(s_x, 16)
            sp.dma_start(cst[:], const).then_inc(s_cst, 16)
            sp.dma_start(rw_s[:], rw).then_inc(s_ffw, 16)
            sp.dma_start(wg_s[:], wg).then_inc(s_ffw, 16)
            sp.dma_start(wd_s[:, 0:FULL, :], wd[0:FULL * P, :].rearrange("(b p) d -> p b d", p=P)).then_inc(s_ffw, 16)
            sp.dma_start(wd_s[0:WIDTH[-1], FULL, :], wd[FULL * P:HID, :]).then_inc(s_ffw, 16)

            def load(u, i, steady):
                sp.wait_ge(s_keep, u)
                sp.dma_start(x_next[:], x[u].rearrange("(j p) d -> p j d", p=P)).then_inc(s_x, 16)

            def store(u, i, steady):
                sp.wait_ge(s_res["f2"], u + 1)
                sp.dma_start(out[u].rearrange("(j p) d -> p j d", p=P), xs["out"][:]).then_inc(s_out, 16)

            def run(i, steady):
                if steady or i >= 0:
                    schedule(i, steady, lambda *a: None, {"f1.load": load, "f2.back2": store})
            iterations(sp, run)
            sp.wait_ge(s_out, 16 * UNITS)

        @block.gpsimd
        def _(pool):
            pool.memset(ones[:], 1.0).then_inc(s_gpc, 1)
            pool.memset(power[:], -0.5).then_inc(s_gpc, 1)
            pool.memset(eps[:], EPS).then_inc(s_gpc, 1)
            for s in ffns:
                pool.memset(ch[s][:].bitcast(F32), 0.0).then_inc(s_gpc, 1)
            pool.wait_ge(s_gpc, 5)

            def stats(s):
                def f(u, i, steady):
                    pool.wait_ge(s_mv[s], u + 1)
                    nc.gpsimd.tensor_tensor(vare[s][:], mv[s][:, :, 1], eps[:], ALU.add).then_inc(s_ve[s], 1)
                    pool.wait_ge(s_ve[s], u + 1)
                    nc.gpsimd.tensor_tensor(rstd[s][:], vare[s][:], power[:], ALU.pow).then_inc(s_rs[s], 1)
                return f

            def weigh(e):
                def f(u, i, steady):
                    if e == 0:
                        pool.wait_ge(s_q, u + 1)
                    pool.wait_ge(s_cum, u * HD + e + 1)
                    if steady or u > 0 or e >= 2:
                        pool.wait_ge(s_o, u * HD + e - 1)
                    nc.gpsimd.tensor_tensor(prod[:, e % 2], cum[:, e % 2], qT[:], ALU.mult).then_inc(s_pr, 1)
                return f

            side = {"f1.stats": stats("f1"), "at.stats": stats("at"), "f2.stats": stats("f2")}
            for e in range(HD):
                side[f"at.p{e}"] = weigh(e)

            def main(i, steady, slot):
                if not (now := block_of(i, steady, slot)):
                    return
                _, _, b, n, w, _ = now
                pool.wait_ge(s_cs, n + 1)
                pool.wait_ge(s_sg, n + 1)
                if not isinstance(n, int) or n >= REUSE:
                    pool.wait_ge(s_h, n - REUSE + 1)
                nc.gpsimd.tensor_tensor(sc[0:w, b % BUFS], sg[0:w, b % BUFS], cs[0:w, b % BUFS],
                                        ALU.mult).then_inc(s_sc, 1)

            def run(i, steady):
                if not steady and i == -1:
                    side["f1.stats"](0, i, steady)
                else:
                    schedule(i, steady, main, side)
            iterations(pool, run)

        @block.scalar
        def _(act):
            act.dma_start(wu_s[:], wu).then_inc(s_ffw, 16)
            act.dma_start(wq_s[:], wq).then_inc(s_atw, 16)
            act.dma_start(wk_s[:], wk).then_inc(s_atw, 16)
            act.dma_start(wv_s[:], wv).then_inc(s_atw, 16)
            act.dma_start(wc_s[:], wc).then_inc(s_atw, 16)
            act.dma_start(lt_s[:], lt).then_inc(s_atw, 16)

            def turn(s):
                def f(u, i, steady):
                    act.wait_ge(s_xt[s], u + 1)
                    if s == "at":
                        if steady or u > 0:
                            act.wait_ge(s_v, u * HD)
                    elif steady or u > 0:
                        act.wait_ge(s_u, last_up(s, u))
                    nc.scalar.activation(xh[s][:], pt[:], ACT.Copy).then_inc(s_xh[s], 1)
                return f

            def tanh(s):
                def f(u, i, steady):
                    act.wait_ge(s_rt[s], u * RT + 4)
                    nc.scalar.activation(th[s][:], th[s][:], ACT.Tanh, scale=0.5).then_inc(s_th[s], 1)
                return f

            def comb(s):
                def f(u, i, steady):
                    act.wait_ge(s_cbp[s], u + 1)
                    if steady or u > 0:
                        act.wait_ge(s_c, last_up(s, u))
                    nc.scalar.activation(cT[s][:], pt[:], ACT.Copy).then_inc(s_cT[s], 1)
                    act.wait_ge(s_cT[s], u + 1)
                    act.sem_inc(s_bank, 1)
                return f

            def back(s):
                def f(u, i, steady):
                    if s == "at":
                        act.wait_ge(s_o, (u + 1) * HD)
                    else:
                        act.wait_ge(s_d, last_up(s, u + 1))
                    if steady or u > 0:
                        act.wait_ge(s_yt[s], u)
                    nc.scalar.activation(yT[s][:], (pa if s == "at" else py)[:], ACT.Copy).then_inc(s_y[s], 1)
                return f

            def keep(u, i, steady):
                act.wait_ge(s_xn["f1"], u + 1)
                if steady or u > 0:
                    act.wait_ge(s_res["f1"], u)
                nc.scalar.activation(xs["f1"][:], x_next[:], ACT.Copy).then_inc(s_keep, 1)

            def keys(u, i, steady):
                act.wait_ge(s_kp, u + 1)
                if steady or u > 0:
                    act.wait_ge(s_kv, u * HD)
                nc.scalar.activation(kT[:], pt[:], ACT.Copy).then_inc(s_k, 1)
                act.wait_ge(s_k, u + 1)
                act.sem_inc(s_bank, 1)

            def queries(u, i, steady):
                act.wait_ge(s_qp, u + 1)
                if steady or u > 0:
                    act.wait_ge(s_pr, u * HD)
                nc.scalar.activation(qT[:], pt[:], ACT.Copy).then_inc(s_q, 1)
                act.wait_ge(s_q, u + 1)
                act.sem_inc(s_bank, 1)

            def main(i, steady, slot):
                if now := block_of(i, steady, slot):
                    _, _, b, n, w, _ = now
                    act.wait_ge(s_g, n + 1)
                    if not isinstance(n, int) or n >= REUSE:
                        act.wait_ge(s_sc, n - REUSE + 1)
                    nc.scalar.activation(sg[0:w, b % BUFS], pg[0:w, :], ACT.Silu).then_inc(s_sg, 1)
                    act.wait_ge(s_c, n + 1)
                    nc.scalar.activation(cs[0:w, b % BUFS], pc[0:w, :], ACT.Copy).then_inc(s_cs, 1)
                if before := block_of(i, steady, slot - 1):
                    _, _, b, n, w, _ = before
                    act.wait_ge(s_h, n + 1)
                    if not isinstance(n, int) or n >= REUSE:
                        act.wait_ge(s_d, n - REUSE + 1)
                    nc.scalar.activation(hh[0:w, b % BUFS], h32[0:w, b % BUFS], ACT.Copy).then_inc(s_hh, 1)

            side = {"at.k": keys, "at.q": queries, "f1.keep": keep}
            for s in stages:
                side[f"{s}.turn"], side[f"{s}.back1"] = turn(s), back(s)
            for s in ffns:
                side[f"{s}.logits"], side[f"{s}.comb"] = tanh(s), comb(s)

            def run(i, steady):
                if not steady and i == -1:
                    act.wait_ge(s_ffw, 16 * 5)
                    for dst, src in ((rw_hl[:, 0, :], rw_s[:]), (wg_h[:], wg_s[:]), (wu_h[:], wu_s[:])):
                        nc.scalar.activation(dst, src, ACT.Copy).then_inc(s_hi, 1)
                    for name in ("turn", "logits", "comb", "keep"):
                        side[f"f1.{name}"](0, i, steady)
                    nc.scalar.activation(wd_h[:, 0:FULL, :], wd_s[:, 0:FULL, :], ACT.Copy).then_inc(s_hi, 1)
                    nc.scalar.activation(wd_h[0:WIDTH[-1], FULL, :], wd_s[0:WIDTH[-1], FULL, :],
                                         ACT.Copy).then_inc(s_hi, 1)
                    act.wait_ge(s_atw, 16 * 5)
                    for dst, src in ((wq_h, wq_s), (wk_h, wk_s)):
                        nc.scalar.activation(dst[:], src[:], ACT.Copy).then_inc(s_hi, 1)
                    nc.scalar.activation(wv_h[:].rearrange("p e (h d) -> p e h d", d=HD), spread_v(),
                                         ACT.Copy).then_inc(s_hi, 1)
                else:
                    schedule(i, steady, main, side)
            iterations(act, run)

        @block.vector
        def _(dve):
            def stats(s):
                def f(u, i, steady):
                    if s == "f1":
                        dve.wait_ge(s_x, 16 * (u + 1))
                    else:
                        dve.wait_ge(s_res["at" if s == "f2" else "f1"], u + 1)
                    for j in range(NT):
                        ins = nc.vector.bn_stats(st6[s][:, j, :], x_read[s][:, j, :])
                    ins.then_inc(s_st6[s], 1)
                    dve.wait_ge(s_st6[s], u + 1)
                    dve.sem_inc(s_agg, 1)
                    for j in range(NT):
                        ins = nc.vector.bn_aggr(mv[s][:, j, :], st6[s][:, j, :])
                    ins.then_inc(s_mv[s], 1)
                return f

            def norm(s):
                def f(u, i, steady):
                    dve.wait_ge(s_rs[s], u + 1)
                    if steady or u > 0:
                        dve.wait_ge(s_xt[s], u)
                    for j in range(NT):
                        ins = nc.vector.tensor_scalar(xn[s][:, j, :], x_read[s][:, j, :], mv[s][:, j, 0:1],
                                                      rstd[s][:, j:j + 1], ALU.subtract, ALU.mult)
                    ins.then_inc(s_xn[s], 1)
                return f

            def turn(s):
                def f(u, i, steady):
                    dve.wait_ge(s_xh[s], u + 1)
                    nc.vector.tensor_tensor(xl[s][:], pt[:], xh[s][:].bitcast(F32), ALU.subtract).then_inc(s_xl[s], 1)
                    dve.wait_ge(s_xl[s], u + 1)
                    dve.sem_inc(s_bank, 1)
                return f

            def logits(s):
                def f(u, i, steady):
                    done = u * RT
                    dve.wait_ge(s_lgp[s], u + 1)
                    nc.vector.reduce_sum(lg[s][:], pt[:, 0:2 * NT * RW].rearrange("p (j t c) -> p j c t", t=2, c=RW),
                                         mybir.AxisListType.X).then_inc(s_rt[s], 1)
                    dve.wait_ge(s_rt[s], done + 1)
                    dve.sem_inc(s_bank, 1)
                    for j in range(NT):
                        ins = nc.vector.max(top[s][:, j, :], lg[s][:, j, 0:NE])
                    ins.then_inc(s_rt[s], 1)
                    dve.wait_ge(s_rt[s], done + 2)
                    nc.vector.tensor_tensor(th[s][:, :, 0], top[s][:, :, 0], top[s][:, :, 1], ALU.subtract).then_inc(s_rt[s], 1)
                    nc.vector.tensor_copy(th[s][:, :, 1], lg[s][:, :, NE]).then_inc(s_rt[s], 1)
                    for j in range(NT):
                        ins = nc.vector.max_index(idx[s][:, j, :], top[s][:, j, :], lg[s][:, j, 0:NE])
                    ins.then_inc(s_rt[s], 1)
                return f

            def weigh(s):
                def f(u, i, steady):
                    done = u * RT + 5
                    dve.wait_ge(s_rt[s], done)
                    nc.vector.tensor_copy(idxf[s][:], idx[s][:, :, 0:2])
                    dve.wait_ge(s_th[s], u + 1)
                    nc.vector.tensor_scalar(w2[s][:, :, 0], th[s][:, :, 0], 0.5, 0.5, ALU.mult, ALU.add)
                    nc.vector.tensor_scalar(w2[s][:, :, 1], th[s][:, :, 0], -0.5, 0.5, ALU.mult, ALU.add)
                    nc.vector.tensor_scalar(cb[s][:, :, NE], th[s][:, :, 1], 0.5, 0.5, ALU.mult,
                                            ALU.add).then_inc(s_rt[s], 1)
                    dve.wait_ge(s_rt[s], done + 1)
                    for k in range(2):
                        ins = nc.vector.tensor_tensor(
                            eq[s][:, k], iota.unsqueeze(1).to_broadcast([P, NT, NE]),
                            idxf[s][:, :, k:k + 1].to_broadcast([P, NT, NE]), ALU.is_equal)
                    ins.then_inc(s_rt[s], 1)
                    dve.wait_ge(s_rt[s], done + 2)
                    for k in range(2):
                        ins = nc.vector.tensor_tensor(
                            eq[s][:, k], eq[s][:, k], w2[s][:, :, k:k + 1].to_broadcast([P, NT, NE]), ALU.mult)
                    ins.then_inc(s_rt[s], 1)
                    dve.wait_ge(s_rt[s], done + 3)
                    nc.vector.tensor_tensor(cb[s][:, :, 0:NE], eq[s][:, 0], eq[s][:, 1], ALU.add).then_inc(s_rt[s], 1)
                    dve.wait_ge(s_rt[s], done + 4)
                    if steady or u > 0:
                        dve.wait_ge(s_cbp[s], u)
                    nc.vector.tensor_copy(ch[s][:, :, 0:NE + 1], cb[s][:]).then_inc(s_hl[s], 1)
                    dve.wait_ge(s_hl[s], 2 * u + 1)
                    nc.vector.tensor_tensor(ch[s][:, :, LO:LO + NE + 1], cb[s][:],
                                            ch[s][:, :, 0:NE + 1].bitcast(F32), ALU.subtract).then_inc(s_hl[s], 1)
                return f

            def back(s):
                after, half = {"f1": ("at", 0.5), "at": ("f2", 1.0), "f2": ("out", 0.5)}[s]

                def f(u, i, steady):
                    if s == "f1":
                        dve.wait_ge(s_keep, u + 1)
                    dve.wait_ge(s_yt[s], u + 1)
                    if steady or u > 0:
                        if s == "f2":
                            dve.wait_ge(s_out, 16 * u)
                        else:
                            dve.wait_ge(s_res[after], u)
                    nc.vector.scalar_tensor_tensor(xs[after][:], tiles(pt[:]), half, xs[s][:],
                                                   ALU.mult, ALU.add).then_inc(s_res[s], 1)
                    dve.wait_ge(s_res[s], u + 1)
                    dve.sem_inc(s_bank, 1)
                return f

            def values(e):
                def f(u, i, steady):
                    if e == 0:
                        dve.wait_ge(s_k, u + 1)
                    dve.wait_ge(s_v, u * HD + e + 1)
                    nc.vector.tensor_tensor(kv[:, e % 2], pv[:], kT[:], ALU.mult).then_inc(s_kv, 1)

                    def scan():
                        dve.wait_ge(s_kv, u * HD + e + 1)
                        if steady or u > 0 or e >= 2:
                            dve.wait_ge(s_pr, u * HD + e - 1)
                        nc.vector.tensor_tensor_scan(cum[:, e % 2], ones[:].to_broadcast([P, TOK]), kv[:, e % 2],
                                                     0.0, ALU.mult, ALU.add).then_inc(s_cum, 1)
                    return scan
                return f

            def main(i, steady, slot):
                if before := block_of(i, steady, slot - 2):
                    _, _, b, n, w, _ = before
                    dve.wait_ge(s_hh, n + 1)
                    nc.vector.tensor_tensor(hl[0:w, b % BUFS], h32[0:w, b % BUFS],
                                            hh[0:w, b % BUFS].bitcast(F32), ALU.subtract).then_inc(s_hlo, 1)
                if before := block_of(i, steady, slot - 1):
                    _, _, b, n, w, par = before
                    dve.wait_ge(s_u, n + 1)
                    dve.wait_ge(s_sc, n + 1)
                    nc.vector.tensor_tensor(h32[0:w, b % BUFS], pu[par][0:w, :], sc[0:w, b % BUFS],
                                            ALU.mult).then_inc(s_h, 1)

            side = {}
            for s in stages:
                side[f"{s}.stats"], side[f"{s}.norm"], side[f"{s}.turn"] = stats(s), norm(s), turn(s)
                side[f"{s}.back2"] = back(s)
            for s in ffns:
                side[f"{s}.logits"], side[f"{s}.weigh"] = logits(s), weigh(s)
            for e in range(HD):
                side[f"at.a{e}"] = values(e)

            def low_half(dst, src, hi, n):
                dve.wait_ge(s_hi, n)
                nc.vector.tensor_tensor(dst, src, hi.bitcast(F32), ALU.subtract).then_inc(s_lo, 1)

            def run(i, steady):
                if not steady and i == -1:
                    dve.wait_ge(s_gpc, 5)
                    side["f1.stats"](0, i, steady)
                    side["f1.norm"](0, i, steady)
                    low_half(rw_hl[:, 1, :], rw_s[:], rw_hl[:, 0, :], 1)
                    side["f1.turn"](0, i, steady)
                    dve.wait_ge(s_cst, 16)
                    side["f1.logits"](0, i, steady)
                    nc.vector.tensor_copy(sel[:], cst[:, C_SEL:C_N]).then_inc(s_lo, 1)
                    side["f1.weigh"](0, i, steady)
                    low_half(wg_l[:], wg_s[:], wg_h[:], 2)
                    low_half(wu_l[:], wu_s[:], wu_h[:], 3)
                    low_half(wd_l[:, 0:FULL, :], wd_s[:, 0:FULL, :], wd_h[:, 0:FULL, :], 4)
                    low_half(wd_l[0:WIDTH[-1], FULL, :], wd_s[0:WIDTH[-1], FULL, :],
                             wd_h[0:WIDTH[-1], FULL, :], 5)
                    dve.wait_ge(s_atw, 16 * 5)
                    nc.vector.tensor_tensor(low[:].rearrange("p (h e) -> p h e", e=HD),
                                            lt_s[:].unsqueeze(1).to_broadcast([P, HEADS, HD]),
                                            cst[:, C_HM:C_HM + P].rearrange("p (h e) -> p h e", e=HD),
                                            ALU.mult).then_inc(s_low, 1)
                    low_half(wq_l[:], wq_s[:], wq_h[:], 6)
                    low_half(wk_l[:], wk_s[:], wk_h[:], 7)
                    dve.wait_ge(s_hi, 8)
                    for e in range(HD):
                        ins = nc.vector.tensor_tensor(
                            wv_l[:, e, :].rearrange("p (h d) -> p h d", d=HD), spread_v()[:, e],
                            wv_h[:, e, :].bitcast(F32).rearrange("p (h d) -> p h d", d=HD), ALU.subtract)
                    ins.then_inc(s_lo, 1)
                    dve.wait_ge(s_bm, 1)
                    nc.vector.tensor_copy(bmix[:], pv[:, 0:P]).then_inc(s_bmc, 1)
                    dve.wait_ge(s_bmc, 1)
                    nc.vector.tensor_copy(
                        mixin[:].rearrange("p e (h d) -> p e h d", d=HD),
                        bmix[:].rearrange("p (h e) -> p e h", e=HD).unsqueeze(3).to_broadcast([P, HD, HEADS, HD]),
                    ).then_inc(s_mixin, 1)
                    for k, bank in enumerate((pv, pa)):
                        dve.wait_ge(s_mx, k + 1)
                        nc.vector.tensor_copy(mix[:, 4 * k:4 * k + 4, :], tiles(bank[:])).then_inc(s_mix, 1)
                else:
                    schedule(i, steady, main, side)
            iterations(dve, run)

        @block.tensor
        def _(pe):
            def three(dst, wh, wl, h, l):
                nc.tensor.matmul(dst, wh, h, start=True, stop=False)
                nc.tensor.matmul(dst, wh, l, start=False, stop=False)
                return nc.tensor.matmul(dst, wl, h, start=False, stop=True)

            def bank(i, steady, name):
                pe.wait_ge(s_bank, uses_before(i, steady, name))

            def turn(s):
                def f(u, i, steady):
                    pe.wait_ge(s_xn[s], u + 1)
                    if steady or i >= 0:
                        bank(i, steady, f"{s}.turn")
                    for j in range(NT):
                        ins = nc.tensor.transpose(pt[:, j * P:(j + 1) * P], xn[s][:, j, :], ident)
                    ins.then_inc(s_xt[s], 1)
                return f

            def logits(s):
                def f(u, i, steady):
                    pe.wait_ge(s_xl[s], u + 1)
                    bank(i, steady, f"{s}.logits")
                    for j in range(NT):
                        h, l = xh[s][:, j * P:(j + 1) * P], xl[s][:, j * P:(j + 1) * P]
                        nc.tensor.matmul(pt[:, 2 * j * RW:2 * (j + 1) * RW], h, rw_hl[:], start=True, stop=True)
                        ins = nc.tensor.matmul(pt[:, 2 * j * RW:(2 * j + 1) * RW], l, rw_hl[:, 0, :],
                                               start=False, stop=True, skip_group_check=True)
                    ins.then_inc(s_lgp[s], 1)
                return f

            def comb(s):
                def f(u, i, steady):
                    pe.wait_ge(s_hl[s], 2 * u + 2)
                    bank(i, steady, f"{s}.comb")
                    for j in range(NT):
                        ins = nc.tensor.transpose(pt[:, j * P:(j + 1) * P], ch[s][:, j, :].bitcast(F32), ident)
                    ins.then_inc(s_cbp[s], 1)
                return f

            def back(s):
                def f(u, i, steady):
                    pe.wait_ge(s_y[s], u + 1)
                    bank(i, steady, f"{s}.back")
                    for j in range(NT):
                        ins = nc.tensor.transpose(pt[:, j * P:(j + 1) * P], yT[s][:, j * P:(j + 1) * P], ident)
                    ins.then_inc(s_yt[s], 1)
                return f

            def keys(u, i, steady):
                pe.wait_ge(s_xl["at"], u + 1)
                bank(i, steady, "at.k")
                three(pt[:], wk_h[:], wk_l[:], xh["at"][:], xl["at"][:]).then_inc(s_kp, 1)

            def queries(u, i, steady):
                bank(i, steady, "at.q")
                three(pt[:], wq_h[:], wq_l[:], xh["at"][:], xl["at"][:]).then_inc(s_qp, 1)

            def values(e):
                def f(u, i, steady):
                    if steady or u > 0 or e > 0:
                        pe.wait_ge(s_kv, u * HD + e)
                    three(pv[:], wv_h[:, e, :], wv_l[:, e, :], xh["at"][:], xl["at"][:]).then_inc(s_v, 1)
                return f

            def mixed(e):
                def f(u, i, steady):
                    pe.wait_ge(s_pr, u * HD + e + 1)
                    if e == 0 and (steady or u > 0):
                        pe.wait_ge(s_y["at"], u)
                    nc.tensor.matmul(pa[:], mix[:, e, :], prod[:, e % 2], start=e == 0,
                                     stop=e == HD - 1).then_inc(s_o, 1)
                return f

            def down(s, u, b, n, w, par):
                pe.wait_ge(s_hlo, n + 1)
                if b == 0 and not (isinstance(n, int) and n == 0):
                    if s == "f1" and isinstance(u, int) and u == 1:
                        pe.wait_ge(s_y["f1"], 1)
                    elif s == "f1":
                        pe.wait_ge(s_y["f2"], u - 1)
                    elif isinstance(u, int) and u == UNITS - 1:
                        pe.wait_ge(s_y["f2"], UNITS - 1)
                    else:
                        pe.wait_ge(s_y["f1"], u + 2)
                h, l = hh[0:w, b % BUFS], hl[0:w, b % BUFS]
                nc.tensor.matmul(py[:], wd_h[0:w, b, :], h, start=b == 0, stop=False)
                nc.tensor.matmul(py[:], wd_h[0:w, b, :], l, start=False, stop=False)
                nc.tensor.matmul(py[:], wd_l[0:w, b, :], h, start=False, stop=b == BLOCKS - 1).then_inc(s_d, 1)

            def up(s, u, b, n, w, par):
                cols = slice(b * P, b * P + w)
                first = isinstance(n, int) and n == 0
                if b == 0:
                    pe.wait_ge(s_xl[s], u + 1)
                if not first:
                    pe.wait_ge(s_sg, n)
                three(pg[0:w, :], wg_h[:, cols], wg_l[:, cols], xh[s][:], xl[s][:]).then_inc(s_g, 1)
                if b == 0:
                    pe.wait_ge(s_cT[s], u + 1)
                if not first:
                    pe.wait_ge(s_cs, n)
                nc.tensor.matmul(pc[0:w, :], sel[:, cols], cT[s][:], start=True, stop=True).then_inc(s_c, 1)
                if not isinstance(n, int) or n >= 2:
                    pe.wait_ge(s_h, n - 1)
                three(pu[par][0:w, :], wu_h[:, cols], wu_l[:, cols], xh[s][:], xl[s][:]).then_inc(s_u, 1)

            def main(i, steady, slot):
                if now := block_of(i, steady, slot):
                    up(*now)
                if before := block_of(i, steady, slot - 3):
                    return lambda: down(*before)

            side = {"at.k": keys, "at.q": queries}
            for s in stages:
                side[f"{s}.turn"], side[f"{s}.back2"] = turn(s), back(s)
            for s in ffns:
                side[f"{s}.logits"], side[f"{s}.comb"] = logits(s), comb(s)
            for e in range(HD):
                side[f"at.a{e}"], side[f"at.b{e}"] = values(e), mixed(e)

            def run(i, steady):
                if not steady and i == -1:
                    pe.wait_ge(s_cst, 16)
                    side["f1.turn"](0, i, steady)
                    pe.wait_ge(s_lo, 1)
                    side["f1.logits"](0, i, steady)
                    side["f1.comb"](0, i, steady)
                    pe.wait_ge(s_low, 1)
                    nc.tensor.matmul(pv[:, 0:P], low[:], low[:], start=True, stop=True).then_inc(s_bm, 1)
                    pe.wait_ge(s_mixin, 1)
                    for k, bank_ in enumerate((pv, pa)):
                        for e in range(4 * k, 4 * k + 4):
                            ins = nc.tensor.matmul(bank_[:, (e % 4) * P:(e % 4 + 1) * P], mixin[:, e, :], wc_s[:],
                                                   start=True, stop=True)
                        ins.then_inc(s_mx, 1)
                    pe.wait_ge(s_lo, 9)
                    pe.wait_ge(s_mix, 2)
                    return
                schedule(i, steady, main, side)
            iterations(pe, run)


_ARGS = ["x", "wg", "wu", "wd", "rw", "wq", "wk", "wv", "wc", "lt", "const"]


def constants():
    c = np.zeros((P, C_N), np.float32)
    c[:, C_ID:C_ID + P] = np.eye(P)
    for h in range(HEADS):
        for k in range(HD):
            for e in range(k, HD):
                c[h * HD + k, C_HM + h * HD + e] = 1.0
    c[:, C_IO:C_IO + NE] = np.arange(NE)
    for m in range(HID):
        k = min(m // FF, NE)
        c[k, C_SEL + m] = c[LO + k, C_SEL + m] = 1.0
    return c


def kernel(L0_attn_X, L0_attn_Wq, L0_attn_Wk, L0_attn_Wv, L0_attn_Wc, L0_attn_Ltri, L0_ffn_gate_w,
           L0_ffn_w_gate_up, L0_ffn_w_down, L0_ffn_shared_w_gate, L0_ffn_shared_w_up,
           L0_ffn_shared_w_down, L0_ffn_shared_gate_w):
    import concourse.bacc as bacc
    from concourse.bass_utils import run_bass_kernel_spmd as run

    gu = np.asarray(L0_ffn_w_gate_up)
    router = np.zeros((P, RW), np.float32)
    router[:, 0:NE] = np.asarray(L0_ffn_gate_w).T
    router[:, NE:NE + 1] = np.asarray(L0_ffn_shared_gate_w).T
    data = [
        np.asarray(L0_attn_X),
        np.concatenate([gu[:, :, 0:FF].transpose(1, 0, 2).reshape(P, -1), np.asarray(L0_ffn_shared_w_gate).T], 1),
        np.concatenate([gu[:, :, FF:].transpose(1, 0, 2).reshape(P, -1), np.asarray(L0_ffn_shared_w_up).T], 1),
        np.concatenate([np.asarray(L0_ffn_w_down).reshape(-1, P), np.asarray(L0_ffn_shared_w_down).T], 0),
        router,
        np.asarray(L0_attn_Wq).T, np.asarray(L0_attn_Wk).T, np.asarray(L0_attn_Wv).T, np.asarray(L0_attn_Wc).T,
        np.asarray(L0_attn_Ltri).transpose(0, 2, 1).reshape(P, HD),
        constants(),
    ]
    nc = bacc.Bacc("TRN2", target_bir_lowering=False, num_devices=1)
    arrays, args = {}, []
    for name, a in zip(_ARGS, data):
        a = np.ascontiguousarray(a)
        arrays[f"in_{name}"] = a
        args.append(nc.dram_tensor(f"in_{name}", a.shape, mybir.dt.from_np(a.dtype), kind="ExternalInput").ap())
    args.append(nc.dram_tensor("out_0", (UNITS, TOK, P), F32, kind="ExternalOutput").ap())
    macaron(nc, *args)
    return run(nc, [arrays], core_ids=[0]).results[0]["out_0"]
```

```python
from contextlib import ExitStack

import numpy as np

import concourse.bass as bass
from concourse import mybir
from concourse.alu_op_type import AluOpType as ALU

F32 = mybir.dt.float32
F32R = mybir.dt.float32r
U32 = mybir.dt.uint32
ACT = mybir.ActivationFunctionType

P = 128
UNITS, TOK = 8, 512
NT = TOK // P
NE, FF, SFF = 16, 64, 352
HID = NE * FF + SFF
BLOCKS = -(-HID // P)
WIDTH = [min(P, HID - P * b) for b in range(BLOCKS)]
FULL = HID // P
SPREAD = NE * FF // P + 1
RW = NE + 2
HEADS, HD = 16, 8
EPS = 1e-5
LO = 64
SLOTS = 2 * BLOCKS
STEADY = 3
BUFS = 4
AT_BUFS = 4
REUSE = 3

HALF_E = HD // 2
ROWS = (slice(0, P // 2), slice(P // 2, P))

C_ID, C_HM, C_IO, C_SEL = 0, P, 2 * P, 2 * P + NE
C_REP = C_SEL + SPREAD * P
C_N = C_REP + HALF_E * P

FRONT = {
    0: [("f1.load", 1), ("at.p3", -1)],
    2: [("f2.copy", -2), ("at.p5", -1)],
    3: [("f2.add", -2), ("at.p6", -1), ("at.p7", -1)],
    4: [("at.copy", -1)],
    12: [("f1.low", 1)],
    13: [("f1.copy", 0)],
    15: [("f1.top", 1)],
    19: [("at.p0", 0)],
    21: [("at.p2", 0)],
}
MIDDLE = {
    5: [("f2.stats", -1)],
    7: [("f2.high", -1)],
    10: [("f2.combT", -1)],
    15: [("f1.tanh", 1)],
    16: [("at.high", 0)],
    17: [("at.kT", 0)],
    20: [("at.p1", 0)],
}
BEHIND = {
    0: [("at.v4", -1), ("at.p4", -1), ("at.b2", -1)],
    1: [("at.v5", -1), ("at.b3", -1)],
    2: [("at.v6", -1), ("at.b4", -1), ("at.v7", -1), ("f2.unturn", -2)],
    3: [("at.b5", -1), ("at.b6", -1), ("at.b7", -1)],
    4: [("at.unturn", -1), ("f1.stats", 1), ("at.add", -1)],
    6: [("f2.norm", -1)],
    7: [("f2.turn", -1), ("f2.low", -1)],
    8: [("f2.logits", -1), ("f2.top", -1), ("f2.tanh", -1), ("f2.index", -1)],
    9: [("f2.pick", -1), ("f2.weigh", -1)],
    10: [("f2.comb", -1), ("f1.norm", 1)],
    11: [("f1.turn", 1), ("f1.high", 1)],
    13: [("f1.unturn", 0), ("f1.add", 0)],
    14: [("f1.logits", 1), ("at.stats", 0)],
    15: [("at.norm", 0)],
    16: [("at.turn", 0), ("at.low", 0), ("f1.index", 1), ("f1.pick", 1)],
    17: [("f1.weigh", 1), ("at.k", 0), ("at.values", 0)],
    18: [("at.q", 0), ("at.qT", 0), ("at.v0", 0)],
    19: [("at.v1", 0), ("f1.keep", 1), ("f1.comb", 1), ("f1.combT", 1)],
    20: [("at.v2", 0), ("at.b0", 0)],
    21: [("at.v3", 0), ("at.b1", 0)],
}

FILL = {0: (11, 12, 13, 14, 15, 16), 1: (5, 6, 7, 9, 10)}
DRAIN = {UNITS - 1: (11, 12, 13, 14, 15, 16), UNITS: (6, 7, 8, 9, 10)}

MOVED = {
    0: [
        ("behind", 5, "f1.norm"), ("behind", 6, "f1.turn"), ("middle", 6, "f1.high"),
        ("behind", 6, "f1.low"), ("behind", 7, "f1.logits"), ("behind", 7, "f1.top"),
        ("middle", 8, "f1.tanh"), ("behind", 8, "f1.index"), ("behind", 8, "f1.pick"),
        ("behind", 8, "f1.weigh"), ("behind", 9, "f1.comb"), ("middle", 9, "f1.combT"),
        ("front", 12, "f1.copy"), ("front", 13, "f1.unturn"), ("front", 13, "f1.add"),
        ("behind", 14, "at.stats"),
    ],
    UNITS: [
        ("front", 13, "f2.copy"), ("behind", 13, "f2.unturn"), ("front", 14, "f2.add"),
    ],
}

BANK_USES = ("turn", "unturn", "logits", "comb", "k", "q")


def places(i, steady):
    lists = {"front": FRONT, "middle": MIDDLE, "behind": BEHIND}
    if steady or i not in MOVED:
        return lists["front"], lists["middle"], lists["behind"]
    offset = {name: off for by_slot in lists.values() for steps in by_slot.values() for name, off in steps}
    moved = [name for _, _, name in MOVED[i]]
    lists = {where: {slot: [step for step in steps if step[0] not in moved] for slot, steps in by_slot.items()}
             for where, by_slot in lists.items()}
    for where, slot, name in MOVED[i]:
        lists[where].setdefault(slot, []).append((name, offset[name]))
    return lists["front"], lists["middle"], lists["behind"]


def bank_uses(i, steady):
    if not steady and i == -1:
        return [("f1.turn", 0), ("f1.logits", 0), ("f1.comb", 0)]
    at = places(i, steady)
    return [(name, i + off) for slot in range(SLOTS) for by_slot in at for name, off in by_slot.get(slot, [])
            if name.split(".")[1] in BANK_USES and (steady or 0 <= i + off < UNITS)]


def use_before(i, steady, name):
    uses = bank_uses(i, steady)
    at = [x for x, _ in uses].index(name)
    if at > 0:
        return uses[at - 1]
    if not steady and i == -1:
        return None
    return bank_uses(i - 1, steady)[-1]


def ffns_before(stage, u):
    if stage == "f1":
        return 0 if isinstance(u, int) and u == 0 else 2 * u - 1
    if isinstance(u, int) and u == UNITS - 1:
        return 2 * u + 1
    return 2 * u + 2


def spread_of(stage, u, b):
    return ffns_before(stage, u) * SPREAD + min(b, SPREAD - 1)


def block_of(i, steady, slot):
    if slot < 0:
        i, slot = i - 1, slot + SLOTS
    stage, unit, b = ("f1", i, slot) if slot < BLOCKS else ("f2", i - 1, slot - BLOCKS)
    if not steady:
        for s, u, spread in (("f1", 1, FILL), ("f2", UNITS - 2, DRAIN)):
            found = [slot_of for it, slots in spread.items() for slot_of in [(it, x) for x in slots]]
            if (i, slot) in found:
                stage, unit, b = s, u, found.index((i, slot))
                break
            if (stage, unit) == (s, u):
                return None
        if not 0 <= unit < UNITS:
            return None
    n = ffns_before(stage, unit) * BLOCKS + b
    return stage, unit, b, n, WIDTH[b], (n if isinstance(n, int) else b + (stage == "f1")) % 2


def macaron(nc, x, wg, wu, wd, rw, wq, wk, wv, wc, lt, const, out):
    ctx = ExitStack()
    with ctx:
        def sb(name, shape, dt=F32):
            return ctx.enter_context(nc.sbuf_tensor(name, shape, dt))

        def pb(name):
            return ctx.enter_context(nc.psum_tensor(name, [P, TOK], F32))

        def sem(name):
            return ctx.enter_context(nc.semaphore(name))

        cst = sb("cst", [P, C_N])
        wg_s, wu_s = sb("wg_s", [P, HID]), sb("wu_s", [P, HID])
        wd_s = sb("wd_s", [P, BLOCKS, P])
        wd_h, wd_l = sb("wd_h", [P, BLOCKS, P], F32R), sb("wd_l", [P, BLOCKS, P], F32R)
        rw_s = sb("rw_s", [P, RW])
        wq_s, wk_s, wv_s, wc_s = (sb(n, [P, P]) for n in ("wq_s", "wk_s", "wv_s", "wc_s"))
        lt_s = sb("lt_s", [P, HD])
        wg_h, wg_l = sb("wg_h", [P, HID], F32R), sb("wg_l", [P, HID], F32R)
        wu_h, wu_l = sb("wu_h", [P, HID], F32R), sb("wu_l", [P, HID], F32R)
        rw_hl = sb("rw_hl", [P, 2, RW], F32R)
        wq_h, wq_l = sb("wq_h", [P, P], F32R), sb("wq_l", [P, P], F32R)
        wk_h, wk_l = sb("wk_h", [P, P], F32R), sb("wk_l", [P, P], F32R)
        wv_h, wv_l = sb("wv_h", [P, 2, P // 2], F32R), sb("wv_l", [P, 2, P // 2], F32R)
        sel = sb("sel", [P, SPREAD * P], F32R)
        rep = sb("rep", [P, HALF_E, P], F32R)
        low = sb("low", [P, P])
        bmix = sb("bmix", [P, P])
        mix = sb("mix", [P, HD, P])
        mixin = sb("mixin", [P, HD, P])
        ones, unused = sb("ones", [P, 1]), sb("unused", [P, 1])
        power, eps = sb("power", [P, NT]), sb("eps", [P, NT])
        ident = cst[:, C_ID:C_ID + P]
        iota = cst[:, C_IO:C_IO + NE]

        xs = {n: sb(f"x_{n}", [P, NT, P]) for n in ("f1", "at", "f2", "out")}
        x_next = sb("x_next", [P, NT, P])
        stages = ("f1", "at", "f2")
        st6 = {s: sb(f"st6_{s}", [P, NT, 6]) for s in stages}
        mv = {s: sb(f"mv_{s}", [P, NT, 2]) for s in stages}
        rstd = {s: sb(f"rstd_{s}", [P, NT]) for s in stages}
        vare = {s: sb(f"vare_{s}", [P, NT]) for s in stages}
        xn = {s: sb(f"xn_{s}", [P, NT, P]) for s in stages}
        xh = {s: sb(f"xh_{s}", [P, TOK], F32R) for s in stages + ("second",)}
        xl = {s: sb(f"xl_{s}", [P, TOK], F32R) for s in stages + ("second",)}
        yT = {s: sb(f"yT_{s}", [P, TOK]) for s in stages}
        ffns = ("f1", "f2")
        lg = {s: sb(f"lg_{s}", [P, NT, RW]) for s in ffns}
        top = {s: sb(f"top_{s}", [P, NT, 8]) for s in ffns}
        idx = {s: sb(f"idx_{s}", [P, NT, 8], U32) for s in ffns}
        idxf = {s: sb(f"idxf_{s}", [P, NT, 2]) for s in ffns}
        th = {s: sb(f"th_{s}", [P, NT, 3]) for s in ffns}
        w2 = {s: sb(f"w2_{s}", [P, NT, 2]) for s in ffns}
        eq = {s: sb(f"eq_{s}", [P, 2 * NT, NE]) for s in ffns}
        cb = {s: sb(f"cb_{s}", [P, NT, NE + 1]) for s in ffns}
        ch = {s: sb(f"ch_{s}", [P, NT, P], F32R) for s in ffns}
        cT = {s: sb(f"cT_{s}", [P, TOK], F32R) for s in ffns + ("second",)}
        cs_shared = sb("cs_shared", [P, TOK])
        sg, cs, sc, h32 = (sb(n, [P, BUFS, TOK]) for n in ("sg", "cs", "sc", "h32"))
        hh, hl = (sb(n, [P, BUFS, TOK], F32R) for n in ("hh", "hl"))
        kT, qT = sb("kT", [P, TOK]), sb("qT", [P, TOK])
        vhl = sb("vhl", [P, 2, TOK], F32R)
        kv = sb("kv", [P, 2, TOK])
        cum, prod = (sb(n, [P, AT_BUFS, TOK]) for n in ("cum", "prod"))

        pg, pc, py, pv, pa, pt = (pb(n) for n in ("pg", "pc", "py", "pv", "pa", "pt"))
        pu = [pb("pu0"), pb("pu1")]

        s_x, s_out, s_idt, s_cst, s_atw = (sem(n) for n in ("x_in", "out_done", "identity_in", "cst_in", "atw_in"))
        s_unused = sem("table_loaded")
        s_gpc, s_sel, s_rep = sem("pool_consts"), sem("sel_ready"), sem("rep_ready")
        split = ("rw", "wg", "wu", "wd", "wq", "wk", "wv")
        s_win = {w: sem(f"{w}_in") for w in split[:4]}
        s_whi = {w: sem(f"{w}_hi") for w in split}
        s_wlo = {w: sem(f"{w}_lo") for w in split}
        s_low, s_bm, s_bmc, s_mixin, s_mx, s_mix = (sem(n) for n in (
            "low_done", "bm_ready", "bmix_done", "mixin_done", "mx_ready", "mix_done"))
        s_g, s_sg, s_u, s_c, s_cs, s_sc, s_h, s_hh, s_hlo, s_d = (sem(n) for n in (
            "gate_ready", "silu_done", "up_ready", "spread_ready", "spread_done", "scaled_done",
            "h_done", "h_hi", "h_lo", "down_done"))
        s_st6 = {s: sem(f"{s}_stats6") for s in stages}
        s_mv = {s: sem(f"{s}_stats") for s in stages}
        s_ve = {s: sem(f"{s}_var") for s in stages}
        s_rs = {s: sem(f"{s}_rstd") for s in stages}
        s_xn = {s: sem(f"{s}_normed") for s in stages}
        s_xt = {s: sem(f"{s}_turned") for s in stages}
        s_xh = {s: sem(f"{s}_hi") for s in stages}
        s_xl = {s: sem(f"{s}_lo") for s in stages}
        s_lgp = {s: sem(f"{s}_logits") for s in ffns}
        s_rt = {s: sem(f"{s}_route") for s in ffns}
        s_keep = sem("input_kept")
        s_agg = sem("aggregate")
        s_hl = {s: sem(f"{s}_halves") for s in ffns}
        s_th = {s: sem(f"{s}_tanh") for s in ffns}
        s_cbp = {s: sem(f"{s}_comb_turned") for s in ffns}
        s_cT = {s: sem(f"{s}_comb_ready") for s in ffns}
        s_y = {s: sem(f"{s}_yT") for s in stages}
        s_yt = {s: sem(f"{s}_y_turned") for s in stages}
        s_res = {s: sem(f"{s}_residual") for s in stages}
        s_kp, s_k, s_qp, s_q = (sem(n) for n in ("k_ready", "k_done", "q_ready", "q_done"))
        s_vp, s_vh, s_vl = sem("values_ready"), sem("values_hi"), sem("values_lo")
        s_v, s_kv, s_cum, s_pr, s_o = (sem(n) for n in (
            "v_ready", "kv_done", "cum_done", "prod_done", "attn_out"))
        RT = 9

        block = ctx.enter_context(nc.Block())

        def tiles(ap):
            return ap.rearrange("p (j c) -> p j c", c=P)

        def iterations(eng, run):
            for i in range(-1, STEADY):
                run(i, False)
            with eng.Fori(STEADY, UNITS - 1) as i:
                run(i, True)
            run(UNITS - 1, False)
            run(UNITS, False)
            run(UNITS + 1, False)

        def schedule(i, steady, side, start=None, main=None, rest=None, end=None):
            front, middle, behind = places(i, steady)

            once = {0: ["down", "keep"], 1: ["downlow"], 2: ["halves"], 3: ["squares", "values"], 4: ["operand"],
                    5: ["mixes"], 6: ["mixed"]}
            if not steady and i == 0:
                behind = dict(behind)
                for slot, steps in once.items():
                    behind[slot] = behind.get(slot, []) + [(f"once.{x}", 0) for x in steps]

            def side_work(steps):
                for name, off in steps:
                    if (steady or 0 <= i + off < UNITS) and name in side:
                        side[name](i + off, i, steady)

            def blocks(part, slot):
                if part:
                    part(i, steady, slot)

            for slot in range(SLOTS):
                blocks(start, slot)
                side_work(front.get(slot, []))
                blocks(main, slot)
                side_work(middle.get(slot, []))
                blocks(rest, slot)
                side_work(behind.get(slot, []))
                blocks(end, slot)

        def group_v():
            return wv_s[:].rearrange("p (h g e) -> p g h e", g=2, e=HALF_E)

        def of_group(w, g):
            return w[:, g, :].rearrange("p (h e) -> p h e", e=HALF_E)

        def last_up(s, u):
            if isinstance(u, int) and u == 0:
                return 0
            return (ffns_before(s, u - 1) + 1) * BLOCKS

        def buffers(s, u):
            if s == "f1" and isinstance(u, int) and u == 1:
                return "second"
            return "f1" if s == "f2" and isinstance(u, int) and u == UNITS - 1 else s

        def residual(s, u):
            return "f1" if s == "f2" and isinstance(u, int) and u == UNITS - 1 else s

        def stage_input(s, u):
            return x_next if s == "f1" else xs[residual(s, u)]

        def spread_in(b):
            return cs[:, b % BUFS] if b < SPREAD - 1 else cs_shared[:]

        def input_used(s, u):
            return last_up("f1", UNITS) if s == "f2" and buffers(s, u) == "f1" else last_up(s, u)

        def weights_used(s, u):
            at, v = ("f1", UNITS - 1) if s == "f2" and buffers(s, u) == "f1" else (s, u - 1)
            return spread_of(at, v, BLOCKS) + 1

        @block.sync
        def _(sp):
            sp.dma_start(x_next[:], x[0].rearrange("(j p) d -> p j d", p=P)).then_inc(s_x, 16)
            sp.dma_start(wg_s[:], wg).then_inc(s_win["wg"], 16)
            sp.dma_start(cst[:, P:C_N], const[:, P:C_N]).then_inc(s_cst, 16)
            sp.dma_start(wd_s[:, 0:FULL, :],
                         wd[0:FULL * P, :].rearrange("(b p) d -> p b d", p=P)).then_inc(s_win["wd"], 16)
            sp.dma_start(wd_s[0:WIDTH[-1], FULL, :], wd[FULL * P:HID, :]).then_inc(s_win["wd"], 16)
            sp.dma_start(wq_s[:], wq).then_inc(s_atw, 16)
            sp.dma_start(wk_s[:], wk).then_inc(s_atw, 16)
            sp.dma_start(wv_s[:], wv).then_inc(s_atw, 16)
            sp.dma_start(wc_s[:], wc).then_inc(s_atw, 16)
            sp.dma_start(lt_s[:], lt).then_inc(s_atw, 16)

            def load(u, i, steady):
                sp.wait_ge(s_keep, u)
                sp.dma_start(x_next[:], x[u].rearrange("(j p) d -> p j d", p=P)).then_inc(s_x, 16)

            def store(u, i, steady):
                sp.wait_ge(s_res["f2"], u + 1)
                sp.dma_start(out[u].rearrange("(j p) d -> p j d", p=P), xs["out"][:]).then_inc(s_out, 16)

            def run(i, steady):
                if steady or i >= 0:
                    schedule(i, steady, {"f1.load": load, "f2.add": store})
            iterations(sp, run)
            sp.wait_ge(s_out, 16 * UNITS)

        @block.gpsimd
        def _(pool):
            pool.memset(ones[:], 1.0).then_inc(s_gpc, 1)
            pool.memset(power[:], -0.5).then_inc(s_gpc, 1)
            pool.memset(eps[:], EPS).then_inc(s_gpc, 1)
            for s in ffns:
                pool.memset(ch[s][:].bitcast(F32), 0.0).then_inc(s_gpc, 1)
            pool.wait_ge(s_gpc, 5)

            def stats(s):
                def f(u, i, steady):
                    pool.wait_ge(s_mv[s], u + 1)
                    nc.gpsimd.tensor_tensor(vare[s][:], mv[s][:, :, 1], eps[:], ALU.add).then_inc(s_ve[s], 1)
                    pool.wait_ge(s_ve[s], u + 1)
                    nc.gpsimd.tensor_tensor(rstd[s][:], vare[s][:], power[:], ALU.pow).then_inc(s_rs[s], 1)
                return f

            def weigh(e):
                def f(u, i, steady):
                    if e == 0:
                        pool.wait_ge(s_q, u + 1)
                    pool.wait_ge(s_cum, u * HD + e + 1)
                    if steady or u > 0 or e >= AT_BUFS:
                        pool.wait_ge(s_o, u * HD + e - AT_BUFS + 1)
                    nc.gpsimd.tensor_tensor(prod[:, e % AT_BUFS], cum[:, e % AT_BUFS], qT[:],
                                            ALU.mult).then_inc(s_pr, 1)
                return f

            side = {f"{s}.stats": stats(s) for s in stages}
            for e in range(HD):
                side[f"at.p{e}"] = weigh(e)

            def main(i, steady, slot):
                if not (now := block_of(i, steady, slot)):
                    return
                s, u, b, n, w, _ = now
                pool.wait_ge(s_cs, spread_of(s, u, b) + 1)
                pool.wait_ge(s_sg, n + 1)
                if not isinstance(n, int) or n >= REUSE:
                    pool.wait_ge(s_h, n - REUSE + 1)
                nc.gpsimd.tensor_tensor(sc[0:w, b % BUFS], sg[0:w, b % BUFS], spread_in(b)[0:w],
                                        ALU.mult).then_inc(s_sc, 1)

            def run(i, steady):
                if not steady and i == -1:
                    side["f1.stats"](0, i, steady)
                    pool.wait_ge(s_whi["wg"], 1)
                    nc.gpsimd.tensor_tensor(wg_l[:], wg_s[:], wg_h[:].bitcast(F32),
                                            ALU.subtract).then_inc(s_wlo["wg"], 1)
                    pool.wait_ge(s_whi["wu"], 1)
                    nc.gpsimd.tensor_tensor(wu_l[:], wu_s[:], wu_h[:].bitcast(F32),
                                            ALU.subtract).then_inc(s_wlo["wu"], 1)
                else:
                    schedule(i, steady, side, main=main)
            iterations(pool, run)

        @block.scalar
        def _(act):
            act.dma_start(cst[:, 0:P], const[:, 0:P]).then_inc(s_idt, 16)
            act.dma_start(rw_s[:], rw).then_inc(s_win["rw"], 16)
            act.dma_start(wu_s[:], wu).then_inc(s_win["wu"], 16)
            act.wait_ge(s_gpc, 5)
            nc.scalar.activation(unused[:], ones[:], ACT.Silu).then_inc(s_unused, 1)

            def turn(s):
                def f(u, i, steady):
                    act.wait_ge(s_xt[s], u + 1)
                    if s == "at":
                        if steady or u > 0:
                            act.wait_ge(s_vp, u)
                    elif steady or (u > 0 and buffers(s, u) != "second"):
                        act.wait_ge(s_u, input_used(s, u))
                    nc.scalar.activation(xh[buffers(s, u)][:], pt[:], ACT.Copy).then_inc(s_xh[s], 1)
                return f

            def tanh(s):
                def f(u, i, steady):
                    act.wait_ge(s_rt[s], u * RT + 3)
                    nc.scalar.activation(th[s][:], th[s][:], ACT.Tanh, scale=0.5).then_inc(s_th[s], 1)
                return f

            def comb(s):
                def f(u, i, steady):
                    act.wait_ge(s_cbp[s], u + 1)
                    if steady or (u > 0 and buffers(s, u) != "second"):
                        act.wait_ge(s_c, weights_used(s, u))
                    nc.scalar.activation(cT[buffers(s, u)][:], pt[:], ACT.Copy).then_inc(s_cT[s], 1)
                return f

            def back(s):
                def f(u, i, steady):
                    if s == "at":
                        act.wait_ge(s_o, (u + 1) * HD)
                    else:
                        act.wait_ge(s_d, last_up(s, u + 1))
                    if steady or u > 0:
                        act.wait_ge(s_yt[s], u)
                    nc.scalar.activation(yT[s][:], (pa if s == "at" else py)[:], ACT.Copy).then_inc(s_y[s], 1)
                return f

            def keep(u, i, steady):
                act.wait_ge(s_xn["f1"], u + 1)
                if steady or u > 0:
                    act.wait_ge(s_res["f1"], u)
                nc.scalar.activation(xs["f1"][:], x_next[:], ACT.Copy).then_inc(s_keep, 1)

            def keys(u, i, steady):
                act.wait_ge(s_kp, u + 1)
                if steady or u > 0:
                    act.wait_ge(s_kv, u * HD)
                nc.scalar.activation(kT[:], pt[:], ACT.Copy).then_inc(s_k, 1)

            def queries(u, i, steady):
                act.wait_ge(s_qp, u + 1)
                if steady or u > 0:
                    act.wait_ge(s_pr, u * HD)
                nc.scalar.activation(qT[:], pt[:], ACT.Copy).then_inc(s_q, 1)

            def main(i, steady, slot):
                if now := block_of(i, steady, slot):
                    s, u, b, n, w, _ = now
                    act.wait_ge(s_g, n + 1)
                    if not isinstance(n, int) or n >= REUSE:
                        act.wait_ge(s_sc, n - REUSE + 1)
                    nc.scalar.activation(sg[0:w, b % BUFS], pg[0:w, :], ACT.Silu).then_inc(s_sg, 1)
                    if b < SPREAD:
                        act.wait_ge(s_c, spread_of(s, u, b) + 1)
                        nc.scalar.activation(spread_in(b), pc[:], ACT.Copy).then_inc(s_cs, 1)

            def rest(i, steady, slot):
                if before := block_of(i, steady, slot - 1):
                    _, _, b, n, w, _ = before
                    act.wait_ge(s_h, n + 1)
                    if not isinstance(n, int) or n >= REUSE:
                        act.wait_ge(s_d, n - REUSE + 1)
                    nc.scalar.activation(hh[0:w, b % BUFS], h32[0:w, b % BUFS], ACT.Copy).then_inc(s_hh, 1)

            def high_half(w, dst, src, loads=1):
                act.wait_ge(s_win[w], 16 * loads)
                nc.scalar.activation(dst, src, ACT.Copy).then_inc(s_whi[w], 1)

            def down_high(u, i, steady):
                high_half("wd", wd_h[:, 0:FULL, :], wd_s[:, 0:FULL, :], 2)
                high_half("wd", wd_h[0:WIDTH[-1], FULL, :], wd_s[0:WIDTH[-1], FULL, :], 2)

            def at_weights(u, i, steady):
                act.wait_ge(s_atw, 16 * 5)
                nc.scalar.activation(wq_h[:], wq_s[:], ACT.Copy).then_inc(s_whi["wq"], 1)
                nc.scalar.activation(wk_h[:], wk_s[:], ACT.Copy).then_inc(s_whi["wk"], 1)
                for g in range(2):
                    ins = nc.scalar.activation(of_group(wv_h, g), group_v()[:, g], ACT.Copy)
                ins.then_inc(s_whi["wv"], 1)
                nc.scalar.activation(rep[:], tiles(cst[:, C_REP:C_N]), ACT.Copy).then_inc(s_rep, 1)

            def mix_operand(u, i, steady):
                act.wait_ge(s_bm, 1)
                nc.scalar.activation(bmix[:], pv[:, 0:P], ACT.Copy).then_inc(s_bmc, 1)
                act.wait_ge(s_bmc, 1)
                nc.scalar.activation(
                    mixin[:].rearrange("p e (h d) -> p e h d", d=HD),
                    bmix[:].rearrange("p (h e) -> p e h", e=HD).unsqueeze(3).to_broadcast([P, HD, HEADS, HD]),
                    ACT.Copy,
                ).then_inc(s_mixin, 1)

            def mix_copy(u, i, steady):
                for k, bank in enumerate((pv, pa)):
                    act.wait_ge(s_mx, k + 1)
                    nc.scalar.activation(mix[:, 4 * k:4 * k + 4, :], tiles(bank[:]), ACT.Copy).then_inc(s_mix, 1)

            def values_high(u, i, steady):
                act.wait_ge(s_vp, u + 1)
                if steady or u > 0:
                    act.wait_ge(s_v, u * HD)
                for g in range(2):
                    nc.scalar.activation(vhl[ROWS[g], g], pv[ROWS[g], :], ACT.Copy).then_inc(s_vh, 1)

            side = {"at.kT": keys, "at.qT": queries, "f1.keep": keep, "once.keep": keep, "once.down": down_high,
                    "once.halves": at_weights, "once.operand": mix_operand, "once.mixed": mix_copy,
                    "at.values": values_high}
            for s in stages:
                side[f"{s}.high"], side[f"{s}.copy"] = turn(s), back(s)
            for s in ffns:
                side[f"{s}.tanh"], side[f"{s}.combT"] = tanh(s), comb(s)

            def run(i, steady):
                if not steady and i == -1:
                    high_half("rw", rw_hl[:, 0, :], rw_s[:])
                    high_half("wg", wg_h[:], wg_s[:])
                    side["f1.high"](0, i, steady)
                    high_half("wu", wu_h[:], wu_s[:])
                    side["f1.tanh"](0, i, steady)
                    act.wait_ge(s_cst, 16)
                    nc.scalar.activation(sel[:], cst[:, C_SEL:C_REP], ACT.Copy).then_inc(s_sel, 1)
                    side["f1.combT"](0, i, steady)
                else:
                    schedule(i, steady, side, main=main, rest=rest)
            iterations(act, run)

        @block.vector
        def _(dve):
            def stats(s):
                def f(u, i, steady):
                    if s == "f1":
                        dve.wait_ge(s_x, 16 * (u + 1))
                    else:
                        dve.wait_ge(s_res["at" if s == "f2" else "f1"], u + 1)
                    for j in range(NT):
                        ins = nc.vector.bn_stats(st6[s][:, j, :], stage_input(s, u)[:, j, :])
                    ins.then_inc(s_st6[s], 1)
                    dve.wait_ge(s_st6[s], u + 1)
                    dve.sem_inc(s_agg, 1)
                    for j in range(NT):
                        ins = nc.vector.bn_aggr(mv[s][:, j, :], st6[s][:, j, :])
                    ins.then_inc(s_mv[s], 1)
                return f

            def norm(s):
                def f(u, i, steady):
                    dve.wait_ge(s_rs[s], u + 1)
                    if steady or u > 0:
                        dve.wait_ge(s_xt[s], u)
                    for j in range(NT):
                        ins = nc.vector.tensor_scalar(xn[s][:, j, :], stage_input(s, u)[:, j, :], mv[s][:, j, 0:1],
                                                      rstd[s][:, j:j + 1], ALU.subtract, ALU.mult)
                    ins.then_inc(s_xn[s], 1)
                return f

            def turn(s):
                def f(u, i, steady):
                    dve.wait_ge(s_xh[s], u + 1)
                    at = buffers(s, u)
                    nc.vector.tensor_tensor(xl[at][:], pt[:], xh[at][:].bitcast(F32),
                                            ALU.subtract).then_inc(s_xl[s], 1)
                return f

            def logits(s):
                def f(u, i, steady):
                    done = u * RT
                    dve.wait_ge(s_lgp[s], u + 1)
                    nc.vector.reduce_sum(lg[s][:], pt[:, 0:2 * NT * RW].rearrange("p (j t c) -> p j c t", t=2, c=RW),
                                         mybir.AxisListType.X).then_inc(s_rt[s], 1)
                    dve.wait_ge(s_rt[s], done + 1)
                    dve.sem_inc(s_agg, 1)
                    for j in range(NT):
                        ins = nc.vector.max(top[s][:, j, :], lg[s][:, j, 0:NE])
                    ins.then_inc(s_rt[s], 1)
                    nc.vector.tensor_copy(th[s][:, :, 2], lg[s][:, :, NE])
                    dve.wait_ge(s_rt[s], done + 2)
                    nc.vector.tensor_tensor(th[s][:, :, 0], top[s][:, :, 0], top[s][:, :, 1], ALU.subtract)
                    nc.vector.tensor_tensor(th[s][:, :, 1], top[s][:, :, 1], top[s][:, :, 0],
                                            ALU.subtract).then_inc(s_rt[s], 1)
                return f

            def index(s):
                def f(u, i, steady):
                    for j in range(NT):
                        ins = nc.vector.max_index(idx[s][:, j, :], top[s][:, j, :], lg[s][:, j, 0:NE])
                    ins.then_inc(s_rt[s], 1)
                return f

            def pick(s):
                def f(u, i, steady):
                    done = u * RT
                    dve.wait_ge(s_rt[s], done + 4)
                    nc.vector.tensor_copy(idxf[s][:], idx[s][:, :, 0:2]).then_inc(s_rt[s], 1)
                    dve.wait_ge(s_rt[s], done + 5)
                    nc.vector.tensor_tensor(
                        eq[s][:], iota.unsqueeze(1).to_broadcast([P, 2 * NT, NE]),
                        idxf[s][:].rearrange("p j k -> p (j k)").unsqueeze(2).to_broadcast([P, 2 * NT, NE]),
                        ALU.is_equal).then_inc(s_rt[s], 1)
                return f

            def weigh(s):
                def f(u, i, steady):
                    done = u * RT + 6
                    dve.wait_ge(s_th[s], u + 1)
                    nc.vector.tensor_scalar(w2[s][:], th[s][:, :, 0:2], 0.5, 0.5, ALU.mult,
                                            ALU.add).then_inc(s_rt[s], 1)
                    nc.vector.tensor_scalar(cb[s][:, :, NE], th[s][:, :, 2], 0.5, 0.5, ALU.mult, ALU.add)
                    dve.wait_ge(s_rt[s], done + 1)
                    nc.vector.tensor_tensor(
                        eq[s][:], eq[s][:],
                        w2[s][:].rearrange("p j k -> p (j k)").unsqueeze(2).to_broadcast([P, 2 * NT, NE]),
                        ALU.mult).then_inc(s_rt[s], 1)
                    dve.wait_ge(s_rt[s], done + 2)
                    by_k = eq[s][:].rearrange("p (j k) e -> p j k e", k=2)
                    nc.vector.tensor_tensor(cb[s][:, :, 0:NE], by_k[:, :, 0, :], by_k[:, :, 1, :],
                                            ALU.add).then_inc(s_rt[s], 1)
                    dve.wait_ge(s_rt[s], done + 3)
                    if steady or u > 0:
                        dve.wait_ge(s_cbp[s], u)
                    nc.vector.tensor_copy(ch[s][:, :, 0:NE + 1], cb[s][:]).then_inc(s_hl[s], 1)
                    dve.wait_ge(s_hl[s], 2 * u + 1)
                    nc.vector.tensor_tensor(ch[s][:, :, LO:LO + NE + 1], cb[s][:],
                                            ch[s][:, :, 0:NE + 1].bitcast(F32), ALU.subtract).then_inc(s_hl[s], 1)
                return f

            def back(s):
                after, half = {"f1": ("at", 0.5), "at": ("f2", 1.0), "f2": ("out", 0.5)}[s]

                def f(u, i, steady):
                    if s == "f1":
                        dve.wait_ge(s_keep, u + 1)
                    dve.wait_ge(s_yt[s], u + 1)
                    if steady or u > 0:
                        if s == "f2":
                            dve.wait_ge(s_out, 16 * u)
                        elif residual(after, u) == after:
                            dve.wait_ge(s_res[after], u)
                    nc.vector.scalar_tensor_tensor(xs[residual(after, u)][:], tiles(pt[:]), half,
                                                   xs[residual(s, u)][:], ALU.mult, ALU.add).then_inc(s_res[s], 1)
                return f

            def values(e):
                def f(u, i, steady):
                    if e == 0:
                        dve.wait_ge(s_k, u + 1)
                    dve.wait_ge(s_v, u * HD + e + 1)
                    nc.vector.tensor_tensor(kv[:, e % 2], pv[:], kT[:], ALU.mult).then_inc(s_kv, 1)
                    dve.wait_ge(s_kv, u * HD + e + 1)
                    if steady or u > 0 or e >= AT_BUFS:
                        dve.wait_ge(s_pr, u * HD + e - AT_BUFS + 1)
                    nc.vector.tensor_tensor_scan(cum[:, e % AT_BUFS], ones[:].to_broadcast([P, TOK]), kv[:, e % 2],
                                                 0.0, ALU.mult, ALU.add).then_inc(s_cum, 1)
                return f

            def start(i, steady, slot):
                if before := block_of(i, steady, slot - 2):
                    _, _, b, n, w, _ = before
                    dve.wait_ge(s_hh, n + 1)
                    nc.vector.tensor_tensor(hl[0:w, b % BUFS], h32[0:w, b % BUFS],
                                            hh[0:w, b % BUFS].bitcast(F32), ALU.subtract).then_inc(s_hlo, 1)

            def main(i, steady, slot):
                if before := block_of(i, steady, slot - 1):
                    _, _, b, n, w, par = before
                    dve.wait_ge(s_u, n + 1)
                    dve.wait_ge(s_sc, n + 1)
                    nc.vector.tensor_tensor(h32[0:w, b % BUFS], pu[par][0:w, :], sc[0:w, b % BUFS],
                                            ALU.mult).then_inc(s_h, 1)

            side = {}
            for s in stages:
                side[f"{s}.stats"], side[f"{s}.norm"], side[f"{s}.low"] = stats(s), norm(s), turn(s)
                side[f"{s}.add"] = back(s)
            for s in ffns:
                side[f"{s}.top"], side[f"{s}.index"] = logits(s), index(s)
                side[f"{s}.pick"], side[f"{s}.weigh"] = pick(s), weigh(s)
            for e in range(HD):
                side[f"at.v{e}"] = values(e)

            def low_half(w, dst, src, hi, n=1):
                dve.wait_ge(s_whi[w], n)
                nc.vector.tensor_tensor(dst, src, hi.bitcast(F32), ALU.subtract).then_inc(s_wlo[w], 1)

            def down_low(u, i, steady):
                low_half("wd", wd_l[:, 0:FULL, :], wd_s[:, 0:FULL, :], wd_h[:, 0:FULL, :])
                low_half("wd", wd_l[0:WIDTH[-1], FULL, :], wd_s[0:WIDTH[-1], FULL, :], wd_h[0:WIDTH[-1], FULL, :], 2)

            def at_weights(u, i, steady):
                dve.wait_ge(s_atw, 16 * 5)
                nc.vector.tensor_tensor(low[:].rearrange("p (h e) -> p h e", e=HD),
                                        lt_s[:].unsqueeze(1).to_broadcast([P, HEADS, HD]),
                                        cst[:, C_HM:C_HM + P].rearrange("p (h e) -> p h e", e=HD),
                                        ALU.mult).then_inc(s_low, 1)
                low_half("wq", wq_l[:], wq_s[:], wq_h[:])
                low_half("wk", wk_l[:], wk_s[:], wk_h[:])

            def at_values(u, i, steady):
                dve.wait_ge(s_whi["wv"], 1)
                for g in range(2):
                    ins = nc.vector.tensor_tensor(of_group(wv_l, g), group_v()[:, g],
                                                  of_group(wv_h, g).bitcast(F32), ALU.subtract)
                ins.then_inc(s_wlo["wv"], 1)

            def values_low(u, i, steady):
                for g in range(2):
                    dve.wait_ge(s_vh, 2 * u + g + 1)
                    nc.vector.tensor_tensor(vhl[ROWS[1 - g], g], pv[ROWS[g], :], vhl[ROWS[g], g].bitcast(F32),
                                            ALU.subtract).then_inc(s_vl, 1)

            side |= {"once.downlow": down_low, "once.halves": at_weights, "once.values": at_values,
                     "at.values": values_low}

            def run(i, steady):
                if not steady and i == -1:
                    dve.wait_ge(s_gpc, 5)
                    side["f1.stats"](0, i, steady)
                    side["f1.norm"](0, i, steady)
                    low_half("rw", rw_hl[:, 1, :], rw_s[:], rw_hl[:, 0, :])
                    side["f1.low"](0, i, steady)
                    dve.wait_ge(s_cst, 16)
                    side["f1.top"](0, i, steady)
                    side["f1.index"](0, i, steady)
                    side["f1.pick"](0, i, steady)
                    side["f1.weigh"](0, i, steady)
                else:
                    schedule(i, steady, side, start=start, main=main)
            iterations(dve, run)

        @block.tensor
        def _(pe):
            def three(dst, wh, wl, h, l):
                nc.tensor.matmul(dst, wh, h, start=True, stop=False)
                nc.tensor.matmul(dst, wh, l, start=False, stop=False)
                return nc.tensor.matmul(dst, wl, h, start=False, stop=True)

            def bank(i, steady, name):
                before = use_before(i, steady, name)
                if before is None:
                    return
                use, u = before
                s, what = use.split(".")
                if what == "unturn":
                    pe.wait_ge(s_res[s], u + 1)
                elif what == "turn":
                    pe.wait_ge(s_xl[s], u + 1)
                elif what == "logits":
                    pe.wait_ge(s_rt[s], u * RT + 1)
                elif what == "comb":
                    pe.wait_ge(s_cT[s], u + 1)
                else:
                    pe.wait_ge(s_k if what == "k" else s_q, u + 1)

            def turn(s):
                def f(u, i, steady):
                    pe.wait_ge(s_xn[s], u + 1)
                    bank(i, steady, f"{s}.turn")
                    for j in range(NT):
                        ins = nc.tensor.transpose(pt[:, j * P:(j + 1) * P], xn[s][:, j, :], ident)
                    ins.then_inc(s_xt[s], 1)
                return f

            def logits(s):
                def f(u, i, steady):
                    pe.wait_ge(s_xl[s], u + 1)
                    bank(i, steady, f"{s}.logits")
                    for j in range(NT):
                        h, l = (x[buffers(s, u)][:, j * P:(j + 1) * P] for x in (xh, xl))
                        nc.tensor.matmul(pt[:, 2 * j * RW:2 * (j + 1) * RW], h, rw_hl[:], start=True, stop=True)
                        ins = nc.tensor.matmul(pt[:, 2 * j * RW:(2 * j + 1) * RW], l, rw_hl[:, 0, :],
                                               start=False, stop=True, skip_group_check=True)
                    ins.then_inc(s_lgp[s], 1)
                return f

            def comb(s):
                def f(u, i, steady):
                    pe.wait_ge(s_hl[s], 2 * u + 2)
                    bank(i, steady, f"{s}.comb")
                    for j in range(NT):
                        ins = nc.tensor.transpose(pt[:, j * P:(j + 1) * P], ch[s][:, j, :].bitcast(F32), ident)
                    ins.then_inc(s_cbp[s], 1)
                return f

            def back(s):
                def f(u, i, steady):
                    pe.wait_ge(s_y[s], u + 1)
                    bank(i, steady, f"{s}.unturn")
                    for j in range(NT):
                        ins = nc.tensor.transpose(pt[:, j * P:(j + 1) * P], yT[s][:, j * P:(j + 1) * P], ident)
                    ins.then_inc(s_yt[s], 1)
                return f

            def keys(u, i, steady):
                pe.wait_ge(s_xl["at"], u + 1)
                if not steady and u == 0:
                    pe.wait_ge(s_wlo["wk"], 1)
                bank(i, steady, "at.k")
                three(pt[:], wk_h[:], wk_l[:], xh["at"][:], xl["at"][:]).then_inc(s_kp, 1)

            def queries(u, i, steady):
                if not steady and u == 0:
                    pe.wait_ge(s_wlo["wq"], 1)
                bank(i, steady, "at.q")
                three(pt[:], wq_h[:], wq_l[:], xh["at"][:], xl["at"][:]).then_inc(s_qp, 1)

            def values(u, i, steady):
                pe.wait_ge(s_xl["at"], u + 1)
                if not steady and u == 0:
                    pe.wait_ge(s_wlo["wv"], 1)
                    pe.wait_ge(s_mix, 2)
                else:
                    pe.wait_ge(s_kv, u * HD)
                w_h, w_l = (w[:].rearrange("p g n -> p (g n)") for w in (wv_h, wv_l))
                three(pv[:], w_h, w_l, xh["at"][:], xl["at"][:]).then_inc(s_vp, 1)

            def spread_value(e):
                def f(u, i, steady):
                    if e == 0:
                        if not steady and u == 0:
                            pe.wait_ge(s_rep, 1)
                        pe.wait_ge(s_vl, 2 * u + 2)
                    else:
                        pe.wait_ge(s_kv, u * HD + e)
                    nc.tensor.matmul(pv[:], rep[:, e % HALF_E, :], vhl[:, e // HALF_E], start=True,
                                     stop=True).then_inc(s_v, 1)
                return f

            def mixed(e):
                def f(u, i, steady):
                    pe.wait_ge(s_pr, u * HD + e + 1)
                    if e == 0 and (steady or u > 0):
                        pe.wait_ge(s_y["at"], u)
                    nc.tensor.matmul(pa[:], mix[:, e, :], prod[:, e % AT_BUFS], start=e == 0,
                                     stop=e == HD - 1).then_inc(s_o, 1)
                return f

            def down(s, u, b, n, w, par):
                pe.wait_ge(s_hlo, n + 1)
                if b == 0 and not (isinstance(n, int) and n == 0):
                    if s == "f1" and isinstance(u, int) and u == 1:
                        pe.wait_ge(s_y["f1"], 1)
                    elif s == "f1":
                        pe.wait_ge(s_y["f2"], u - 1)
                    elif isinstance(u, int) and u == UNITS - 1:
                        pe.wait_ge(s_y["f2"], UNITS - 1)
                    else:
                        pe.wait_ge(s_y["f1"], u + 2)
                if isinstance(n, int) and n == 0:
                    pe.wait_ge(s_wlo["wd"], 2)
                h, l = hh[0:w, b % BUFS], hl[0:w, b % BUFS]
                nc.tensor.matmul(py[:], wd_h[0:w, b, :], h, start=b == 0, stop=False)
                nc.tensor.matmul(py[:], wd_h[0:w, b, :], l, start=False, stop=False)
                nc.tensor.matmul(py[:], wd_l[0:w, b, :], h, start=False, stop=b == BLOCKS - 1).then_inc(s_d, 1)

            def gate(s, u, b, n, w, par):
                if b == 0:
                    pe.wait_ge(s_xl[s], u + 1)
                if isinstance(n, int) and n == 0:
                    pe.wait_ge(s_wlo["wg"], 1)
                else:
                    pe.wait_ge(s_sg, n)
                cols = slice(b * P, b * P + w)
                h, l = (x[buffers(s, u)][:] for x in (xh, xl))
                three(pg[0:w, :], wg_h[:, cols], wg_l[:, cols], h, l).then_inc(s_g, 1)

            def spread(s, u, b, n, w, par):
                if b >= SPREAD:
                    return
                if b == 0:
                    pe.wait_ge(s_cT[s], u + 1)
                if isinstance(n, int) and n == 0:
                    pe.wait_ge(s_sel, 1)
                else:
                    pe.wait_ge(s_cs, spread_of(s, u, b))
                nc.tensor.matmul(pc[:], sel[:, b * P:(b + 1) * P], cT[buffers(s, u)][:], start=True,
                                 stop=True).then_inc(s_c, 1)

            def up(s, u, b, n, w, par):
                if not isinstance(n, int) or n >= 2:
                    pe.wait_ge(s_h, n - 1)
                if isinstance(n, int) and n == 0:
                    pe.wait_ge(s_wlo["wu"], 1)
                cols = slice(b * P, b * P + w)
                h, l = (x[buffers(s, u)][:] for x in (xh, xl))
                three(pu[par][0:w, :], wu_h[:, cols], wu_l[:, cols], h, l).then_inc(s_u, 1)

            def main(i, steady, slot):
                if now := block_of(i, steady, slot):
                    n = now[3]
                    for part in (spread,) if isinstance(n, int) and n == 0 else (gate, spread, up):
                        part(*now)

            def end(i, steady, slot):
                if before := block_of(i, steady, slot - 2):
                    down(*before)

            def squares(u, i, steady):
                pe.wait_ge(s_low, 1)
                nc.tensor.matmul(pv[:, 0:P], low[:], low[:], start=True, stop=True).then_inc(s_bm, 1)

            def mixes(u, i, steady):
                pe.wait_ge(s_mixin, 1)
                for k, half in enumerate((pv, pa)):
                    for e in range(4 * k, 4 * k + 4):
                        ins = nc.tensor.matmul(half[:, (e % 4) * P:(e % 4 + 1) * P], mixin[:, e, :], wc_s[:],
                                               start=True, stop=True)
                    ins.then_inc(s_mx, 1)

            side = {"at.k": keys, "at.q": queries, "once.squares": squares, "once.mixes": mixes,
                    "at.values": values}
            for s in stages:
                side[f"{s}.turn"], side[f"{s}.unturn"] = turn(s), back(s)
            for s in ffns:
                side[f"{s}.logits"], side[f"{s}.comb"] = logits(s), comb(s)
            for e in range(HD):
                side[f"at.v{e}"], side[f"at.b{e}"] = spread_value(e), mixed(e)

            def run(i, steady):
                if not steady and i == -1:
                    pe.wait_ge(s_idt, 16)
                    turn("f1")(0, i, steady)
                    pe.wait_ge(s_wlo["rw"], 1)
                    logits("f1")(0, i, steady)
                    gate(*block_of(0, False, 0))
                    comb("f1")(0, i, steady)
                    up(*block_of(0, False, 0))
                    return
                schedule(i, steady, side, main=main, end=end)
            iterations(pe, run)


_ARGS = ["x", "wg", "wu", "wd", "rw", "wq", "wk", "wv", "wc", "lt", "const"]


def constants():
    c = np.zeros((P, C_N), np.float32)
    c[:, C_ID:C_ID + P] = np.eye(P)
    for h in range(HEADS):
        for k in range(HD):
            for e in range(k, HD):
                c[h * HD + k, C_HM + h * HD + e] = 1.0
    c[:, C_IO:C_IO + NE] = np.arange(NE)
    for m in range(SPREAD * P):
        k = min(m // FF, NE)
        c[k, C_SEL + m] = c[LO + k, C_SEL + m] = 1.0
    for h in range(HEADS):
        for e in range(HALF_E):
            at = C_REP + e * P + h * HD
            for row in (h * HALF_E + e, LO + h * HALF_E + e):
                c[row, at:at + HD] = 1.0
    return c


def kernel(L0_attn_X, L0_attn_Wq, L0_attn_Wk, L0_attn_Wv, L0_attn_Wc, L0_attn_Ltri, L0_ffn_gate_w,
           L0_ffn_w_gate_up, L0_ffn_w_down, L0_ffn_shared_w_gate, L0_ffn_shared_w_up,
           L0_ffn_shared_w_down, L0_ffn_shared_gate_w):
    import concourse.bacc as bacc
    from concourse.bass_utils import run_bass_kernel_spmd as run

    gu = np.asarray(L0_ffn_w_gate_up)
    router = np.zeros((P, RW), np.float32)
    router[:, 0:NE] = np.asarray(L0_ffn_gate_w).T
    router[:, NE:NE + 1] = np.asarray(L0_ffn_shared_gate_w).T
    data = [
        np.asarray(L0_attn_X),
        np.concatenate([gu[:, :, 0:FF].transpose(1, 0, 2).reshape(P, -1), np.asarray(L0_ffn_shared_w_gate).T], 1),
        np.concatenate([gu[:, :, FF:].transpose(1, 0, 2).reshape(P, -1), np.asarray(L0_ffn_shared_w_up).T], 1),
        np.concatenate([np.asarray(L0_ffn_w_down).reshape(-1, P), np.asarray(L0_ffn_shared_w_down).T], 0),
        router,
        np.asarray(L0_attn_Wq).T, np.asarray(L0_attn_Wk).T, np.asarray(L0_attn_Wv).T, np.asarray(L0_attn_Wc).T,
        np.asarray(L0_attn_Ltri).transpose(0, 2, 1).reshape(P, HD),
        constants(),
    ]
    nc = bacc.Bacc("TRN2", target_bir_lowering=False, num_devices=1)
    arrays, args = {}, []
    for name, a in zip(_ARGS, data):
        a = np.ascontiguousarray(a)
        arrays[f"in_{name}"] = a
        args.append(nc.dram_tensor(f"in_{name}", a.shape, mybir.dt.from_np(a.dtype), kind="ExternalInput").ap())
    args.append(nc.dram_tensor("out_0", (UNITS, TOK, P), F32, kind="ExternalOutput").ap())
    macaron(nc, *args)
    return run(nc, [arrays], core_ids=[0]).results[0]["out_0"]
```
